# Optimizing a Trainium2 kernel written in Bass

```python
import numpy as np
import jax
import jax.numpy as jnp

def _softmax(x, axis=-1):
    return jax.nn.softmax(x, axis=axis)

def _gelu(x):
    return jax.nn.gelu(x, approximate=True)

def _silu(x):
    return jax.nn.silu(x)

def _sigmoid(x):
    return jax.nn.sigmoid(x)

def _layernorm(x, axis=-1, eps=1e-05):
    m = jnp.mean(x, axis=axis, keepdims=True)
    v = jnp.var(x, axis=axis, keepdims=True)
    return (x - m) / jnp.sqrt(v + eps)

def _scatter_add(tgt, idx, src, axis=0):
    return tgt.at[idx].add(src)

def _segment_sum(src, seg, n):
    return jax.ops.segment_sum(src, seg, n)
kernel_name = 'mk_decoder_postln_d1_seqx_r8_fe9baf'

def setup_inputs(seed: int=0):
    np.random.seed(seed)
    _w = jnp.asarray

    def _rec_inputs():
        import jax
        import jax.numpy as jnp
        _rk = jax.random.key(seed)
        x = 7.22e-05 + 1 * jax.random.normal(jax.random.fold_in(_rk, 1), (16, 64, 512), jnp.float32)
        _lenS = 64 - jax.random.randint(jax.random.fold_in(_rk, 7), (16,), 0, max(1, 64 // 4) + 1, jnp.int32)
        _lenS2 = 64 - jax.random.randint(jax.random.fold_in(_rk, 8), (16,), 0, max(1, 64 // 4) + 1, jnp.int32)
        _ctx_4096P = jax.random.normal(jax.random.fold_in(_rk, 11), (16, 16, 512), jnp.float32)
        _ctx_4096c = jax.random.dirichlet(jax.random.fold_in(_rk, 511), 0.3 * jnp.ones((16,), jnp.float32), (16, 64))
        _ctx_4096t = jnp.einsum('bsk,bkd->bsd', _ctx_4096c, _ctx_4096P)
        _ctx_4096t = _ctx_4096t * jax.lax.rsqrt(jnp.mean(jnp.square(_ctx_4096t)) + 1e-12) * 0.953939
        ctx_4096 = 4.13588e-05 + 0.999923 * (_ctx_4096t + 0.3 * jax.random.normal(jax.random.fold_in(_rk, 611), (16, 64, 512), jnp.float32))
        return (x, ctx_4096)
    x, ctx_4096 = _rec_inputs()

    def _L0_attn_setup():
        import jax, jax.numpy as jnp
        import numpy as np
        D_MODEL = 512
        N_HEADS = 32
        HEAD_DIM = D_MODEL // N_HEADS
        CLIP_QKV = 8.0
        ALIBI_BIAS_MAX = 8.0
        LN_EPS = 1e-05

        def _alibi_slopes(n_heads: int, bias_max: float) -> jnp.ndarray:
            next_pow2 = 2 ** int(np.ceil(np.log2(n_heads)))
            m = np.arange(1, next_pow2 + 1, dtype=np.float32) * (bias_max / next_pow2)
            slopes = 1.0 / np.power(2.0, m)
            if next_pow2 != n_heads:
                slopes = np.concatenate([slopes[1::2], slopes[::2]])[:n_heads]
            return jnp.asarray(slopes)

        def _layer_norm(x, w, b):
            mu = jnp.mean(x, axis=-1, keepdims=True)
            var = jnp.mean(jnp.square(x - mu), axis=-1, keepdims=True)
            return (x - mu) * jax.lax.rsqrt(var + LN_EPS) * w + b
        key = jax.random.key(seed)
        ks = jax.random.split(key, 3)
        B, S = (1, 256)
        hidden_states = jax.random.normal(ks[0], (B, S, D_MODEL), dtype=jnp.float32)
        Wqkv = jax.random.normal(ks[1], (3 * D_MODEL, D_MODEL), dtype=jnp.float32) * 0.02
        Wout = jax.random.normal(ks[2], (D_MODEL, D_MODEL), dtype=jnp.float32) * 0.02
        return {'hidden_states': hidden_states, 'Wqkv': Wqkv, 'q_ln_w': jnp.ones((D_MODEL,), jnp.float32), 'q_ln_b': jnp.zeros((D_MODEL,), jnp.float32), 'k_ln_w': jnp.ones((D_MODEL,), jnp.float32), 'k_ln_b': jnp.zeros((D_MODEL,), jnp.float32), 'Wout': Wout}
    _L0_attn_all = _L0_attn_setup()
    _L0_attn_in = {k: v for k, v in _L0_attn_all.items() if k in ('Wqkv', 'q_ln_w', 'q_ln_b', 'k_ln_w', 'k_ln_b', 'Wout')}
    del _L0_attn_all

    def _L0_xattn_setup():
        import jax, jax.numpy as jnp
        import numpy as np
        B, S, D = (1, 256, 512)
        H, HKV, DK, DV = (32, 8, 128, 128)
        key = jax.random.key(seed)
        ks = jax.random.split(key, 7)
        std = 0.02
        return {'q': jax.random.normal(ks[0], (B, S, D), jnp.float32), 'k': jax.random.normal(ks[1], (B, S, D), jnp.float32), 'v': jax.random.normal(ks[2], (B, S, D), jnp.float32), 'Wq': jax.random.normal(ks[3], (H * DK, D), jnp.float32) * std, 'Wk': jax.random.normal(ks[4], (HKV * DK, D), jnp.float32) * std, 'Wv': jax.random.normal(ks[5], (HKV * DV, D), jnp.float32) * std, 'Wd': jax.random.normal(ks[6], (D, H * DV), jnp.float32) * std}
    _L0_xattn_all = _L0_xattn_setup()
    _L0_xattn_in = {k: v for k, v in _L0_xattn_all.items() if k in ('Wq', 'Wk', 'Wv', 'Wd')}
    del _L0_xattn_all

    def _L0_ffn_setup():
        import jax, jax.numpy as jnp
        import numpy as np
        TOP_K = 2
        key = jax.random.key(seed)
        k0, k1, k2 = jax.random.split(key, 3)
        B, S, D, H, E = (4, 256, 512, 512, 8)
        sc = 1.0 / np.sqrt(D).astype(np.float32)
        x = jax.random.normal(k0, (B, S, D), dtype=jnp.float32)
        W_gate = jax.random.normal(k1, (D, E), dtype=jnp.float32) * sc
        b_gate = jnp.zeros((E,), dtype=jnp.float32)
        W_e = jax.random.normal(k2, (E, D, H), dtype=jnp.float32) * sc
        b_e = jnp.zeros((E, H), dtype=jnp.float32)
        return {'x': x, 'W_gate': W_gate, 'b_gate': b_gate, 'W_e': W_e, 'b_e': b_e}
    _L0_ffn_all = _L0_ffn_setup()
    _L0_ffn_in = {k: v for k, v in _L0_ffn_all.items() if k in ('W_gate', 'b_gate', 'W_e', 'b_e')}
    del _L0_ffn_all
    return {'x': x, 'ctx_4096': ctx_4096, 'L0_attn_Wqkv': _L0_attn_in['Wqkv'], 'L0_attn_q_ln_w': _L0_attn_in['q_ln_w'], 'L0_attn_q_ln_b': _L0_attn_in['q_ln_b'], 'L0_attn_k_ln_w': _L0_attn_in['k_ln_w'], 'L0_attn_k_ln_b': _L0_attn_in['k_ln_b'], 'L0_attn_Wout': _L0_attn_in['Wout'], 'L0_xattn_Wq': _L0_xattn_in['Wq'], 'L0_xattn_Wk': _L0_xattn_in['Wk'], 'L0_xattn_Wv': _L0_xattn_in['Wv'], 'L0_xattn_Wd': _L0_xattn_in['Wd'], 'L0_ffn_W_gate': _L0_ffn_in['W_gate'], 'L0_ffn_b_gate': _L0_ffn_in['b_gate'], 'L0_ffn_W_e': _L0_ffn_in['W_e'], 'L0_ffn_b_e': _L0_ffn_in['b_e']}

def reference(x, ctx_4096, L0_attn_Wqkv, L0_attn_q_ln_w, L0_attn_q_ln_b, L0_attn_k_ln_w, L0_attn_k_ln_b, L0_attn_Wout, L0_xattn_Wq, L0_xattn_Wk, L0_xattn_Wv, L0_xattn_Wd, L0_ffn_W_gate, L0_ffn_b_gate, L0_ffn_W_e, L0_ffn_b_e):
    import jax
    import jax.numpy as jnp

    def _L0_attn_ref(hidden_states, Wqkv, q_ln_w, q_ln_b, k_ln_w, k_ln_b, Wout):
        import jax, jax.numpy as jnp
        import numpy as np
        D_MODEL = 512
        N_HEADS = 32
        HEAD_DIM = D_MODEL // N_HEADS
        CLIP_QKV = 8.0
        ALIBI_BIAS_MAX = 8.0
        LN_EPS = 1e-05

        def _alibi_slopes(n_heads: int, bias_max: float) -> jnp.ndarray:
            next_pow2 = 2 ** int(np.ceil(np.log2(n_heads)))
            m = np.arange(1, next_pow2 + 1, dtype=np.float32) * (bias_max / next_pow2)
            slopes = 1.0 / np.power(2.0, m)
            if next_pow2 != n_heads:
                slopes = np.concatenate([slopes[1::2], slopes[::2]])[:n_heads]
            return jnp.asarray(slopes)

        def _layer_norm(x, w, b):
            mu = jnp.mean(x, axis=-1, keepdims=True)
            var = jnp.mean(jnp.square(x - mu), axis=-1, keepdims=True)
            return (x - mu) * jax.lax.rsqrt(var + LN_EPS) * w + b
        B, S, _ = hidden_states.shape
        qkv = jnp.einsum('bsd,ed->bse', hidden_states, Wqkv)
        qkv = jnp.clip(qkv, -CLIP_QKV, CLIP_QKV)
        q, k, v = jnp.split(qkv, [D_MODEL, 2 * D_MODEL], axis=-1)
        q = _layer_norm(q, q_ln_w, q_ln_b)
        k = _layer_norm(k, k_ln_w, k_ln_b)
        q = q.reshape(B, S, N_HEADS, HEAD_DIM)
        k = k.reshape(B, S, N_HEADS, HEAD_DIM)
        v = v.reshape(B, S, N_HEADS, HEAD_DIM)
        scale = HEAD_DIM ** (-0.5)
        scores = jnp.einsum('bqhd,bkhd->bhqk', q, k) * scale
        slopes = _alibi_slopes(N_HEADS, ALIBI_BIAS_MAX)
        pos = jnp.arange(S)
        rel = (pos[None, :] - pos[:, None]).astype(jnp.float32)
        scores = scores + slopes[None, :, None, None] * rel[None, None]
        causal = pos[None, :] <= pos[:, None]
        scores = jnp.where(causal[None, None], scores, jnp.float32(-1e+30))
        probs = jax.nn.softmax(scores, axis=-1)
        out = jnp.einsum('bhqk,bkhd->bqhd', probs, v).reshape(B, S, D_MODEL)
        return jnp.einsum('bsd,ed->bse', out, Wout)

    def _L0_xattn_ref(q, k, v, Wq, Wk, Wv, Wd):
        import jax, jax.numpy as jnp
        import numpy as np
        B, S, D = (1, 256, 512)
        H, HKV, DK, DV = (32, 8, 128, 128)
        b, s, _ = q.shape
        exp = H // HKV
        Q = (q @ Wq.T).reshape(b, s, HKV, exp, DK)
        K = (k @ Wk.T).reshape(b, s, HKV, DK)
        V = (v @ Wv.T).reshape(b, s, HKV, DV)
        scale = DK ** (-0.5)
        scores = jnp.einsum('bqhed,bkhd->bheqk', Q, K) * scale
        causal = jnp.tril(jnp.ones((s, s), dtype=bool))
        scores = jnp.where(causal, scores, jnp.finfo(scores.dtype).min)
        probs = jax.nn.softmax(scores, axis=-1)
        attn = jnp.einsum('bheqk,bkhd->bqhed', probs, V)
        attn = attn.reshape(b, s, H * DV)
        return attn @ Wd.T

    def _L0_ffn_ref(x, W_gate, b_gate, W_e, b_e):
        import jax, jax.numpy as jnp
        import numpy as np
        TOP_K = 2
        logits = x @ W_gate + b_gate
        _, top_idx = jax.lax.top_k(logits, TOP_K)
        y_all = jax.nn.relu(jnp.einsum('bsd,edh->bseh', x, W_e) + b_e)
        y = jnp.take_along_axis(y_all, top_idx[..., None], axis=2)
        return y.mean(axis=2)
    x = _layernorm(x + _L0_attn_ref(x, L0_attn_Wqkv, L0_attn_q_ln_w, L0_attn_q_ln_b, L0_attn_k_ln_w, L0_attn_k_ln_b, L0_attn_Wout), axis=-1)
    x = _layernorm(x + _L0_xattn_ref(x, ctx_4096, ctx_4096, L0_xattn_Wq, L0_xattn_Wk, L0_xattn_Wv, L0_xattn_Wd), axis=-1)
    x = _layernorm(x + _L0_ffn_ref(x, L0_ffn_W_gate, L0_ffn_b_gate, L0_ffn_W_e, L0_ffn_b_e), axis=-1)
    return x

_drawn_inputs = setup_inputs


def setup_inputs(seed=0):
    import zlib

    import numpy as np

    out = dict(_drawn_inputs(seed))
    spreads = {'L0_attn_q_ln_w': (1.0, 0.2),
     'L0_attn_q_ln_b': (0.0, 0.1),
     'L0_attn_k_ln_w': (1.0, 0.2),
     'L0_attn_k_ln_b': (0.0, 0.1),
     'L0_ffn_b_gate': (0.0, 0.1),
     'L0_ffn_b_e': (0.0, 0.1)}
    factors = {}
    for name, (base, spread) in spreads.items():
        noise = np.random.default_rng([zlib.crc32(name.encode()), seed]).standard_normal(out[name].shape)
        drawn = base * np.exp(spread * noise) if base else spread * noise
        out[name] = jnp.asarray(drawn.astype(out[name].dtype))
    for name, factor in factors.items():
        out[name] = (out[name] * factor).astype(out[name].dtype)
    return out
```

```python
from contextlib import ExitStack

import concourse.bass as bass
from concourse import mybir

F32 = mybir.dt.float32
F32R = mybir.dt.float32r
I32 = mybir.dt.int32
ALU = mybir.AluOpType
ACT = mybir.ActivationFunctionType
AX = mybir.AxisListType

P = 128
B, S, D = 16, 64, 512
TOK = B * S
NT = TOK // P
C = D // P
NH, HD = 32, 16
HPC = P // HD
G, HG, DK = 8, 4, 128
HALF = TOK // 2
TH = NT // 2
E = 8
CLIP = 8.0
EPS = 1e-5
RING = 5
RING_A = 3
RSQRT_MAGIC = 1597463007.0
RSQRT_OPS = 2 + 3 * 3


class Chain:

    def __init__(self, eng, sem, base):
        self.eng, self.sem, self.base, self.k = eng, sem, base, 0

    def link(self, ins):
        self.k += 1
        ins.then_inc(self.sem, 1)
        self.eng.wait_ge(self.sem, self.base + self.k)


def wait(eng, sem, value):
    if not isinstance(value, int) or value > 0:
        eng.wait_ge(sem, value)


def products(nc, out, lhs, rhs, start=True, stop=True):
    (lh, ll), (rh, rl) = lhs, rhs
    nc.tensor.matmul(out, ll, rh, start=start, stop=False)
    nc.tensor.matmul(out, lh, rl, start=False, stop=False)
    return nc.tensor.matmul(out, lh, rh, start=False, stop=stop)


def rsqrt(nc, chain, var, y, t):
    chain.link(nc.vector.tensor_scalar(var, var, EPS, None, ALU.add))
    chain.link(nc.vector.tensor_scalar(y.bitcast(I32), var.bitcast(I32), -0.5, RSQRT_MAGIC, ALU.mult, ALU.add))
    for _ in range(3):
        chain.link(nc.vector.tensor_tensor(t, y, y, ALU.mult))
        chain.link(nc.vector.scalar_tensor_tensor(t, t, -0.5, var, ALU.mult, ALU.mult))
        chain.link(nc.vector.scalar_tensor_tensor(y, t, 1.5, y, ALU.add, ALU.mult))


def self_attention(nc, top, x_rows, x_cols, w_qkv, w_out, ln_cols, alibi_bias, head_rows):
    with ExitStack() as ctx:
        def sb(name, shape, dt=F32):
            return ctx.enter_context(nc.sbuf_tensor(name, shape, dt))

        def split(name, shape):
            return sb(name + "_hi", shape, F32R), sb(name + "_lo", shape, F32R)

        def sem(name):
            return ctx.enter_context(nc.semaphore(name))

        x_tok, ident = top["x_tok"], top["ident"]
        raw = sb("a_raw", [P, RING_A, D])
        wqkv = split("wqkv", [P, 3 * C, D])
        wout = split("wout", [P, C, D])
        xt_raw = sb("xt_raw", [P, C, P])
        xt = split("xt", [P, C, P])
        qk_tok = sb("qk_tok", [P, 2, D])
        qk_col = sb("qk_col", [P, 2, C, P])
        v_tok = sb("v_tok", [P, 2, D])
        qz = split("qz", [P, C, 2, P])
        kblk = split("kblk", [P, C, 2, HPC, S])
        vblk = split("vblk", [P, 2, C, HPC // 2, P])
        probs = sb("probs", [P, NH, S])
        pt = split("pt", [P, 2, HPC // 2, P])
        ot = split("ot", [P, C, P])
        bias = sb("alibi", [P, NH, S])
        heads = sb("heads", [P, HPC])
        lnp = sb("lnp", [P, 4, C])
        st6 = sb("st6", [P, 2, 6])
        mv = sb("mv", [P, 2, 2])
        rstd = sb("rstd", [P, 2])
        tmp2 = sb("tmp2", [P, 2])
        mx = sb("mx", [P, NH])
        den = sb("den", [P, NH])

        def ps(name):
            return ctx.enter_context(nc.psum_tensor(name, [P, D], F32))

        R = [ps("aR0"), ps("aR1")]
        SC = [ps("aS0"), ps("aS1")]
        T = [ps("aT0"), ps("aT1")]
        O = ps("aO")
        Y = ps("aY")

        raw_in = [sem(f"raw_in{i}") for i in range(RING_A)]
        w_hi = sem("w_hi")
        w_lo = sem("w_lo")
        x_in = sem("x_in")
        par_in = sem("par_in")
        xt_in = sem("xt_in")
        xt_hi = sem("xt_hi")
        xt_lo = sem("xt_lo")
        zeroed = sem("zeroed")
        ident_z = sem("ident_z")
        ident_in = sem("ident_in")
        qkv_done = sem("qkv_done")
        clipped = sem("clipped")
        v_swapped = sem("v_swapped")
        qk_normed = sem("qk_normed")
        qkt_done = sem("qkt_done")
        q_affine = sem("q_affine")
        k_affine = sem("k_affine")
        qz_hi = sem("qz_hi")
        qz_lo = sem("qz_lo")
        k_split = sem("k_split")
        kblk_hi = sem("kblk_hi")
        kblk_lo = sem("kblk_lo")
        vblk_hi = sem("vblk_hi")
        vblk_lo = sem("vblk_lo")
        scores_done = sem("scores_done")
        masked = sem("masked")
        row_max = sem("row_max")
        shifted = sem("shifted")
        exp_done = sem("exp_done")
        inverse = sem("inverse")
        probs_done = sem("probs_done")
        pt_done = sem("pt_done")
        pt_hi = sem("pt_hi")
        pt_lo = sem("pt_lo")
        pv_done = sem("pv_done")
        ot_hi = sem("ot_hi")
        ot_lo = sem("ot_lo")
        y_done = sem("y_done")
        y_added = sem("y_added")
        step_n = sem("a_step_n")
        step_i = sem("a_step_i")

        def vblk_diag(a, b, h):
            flat = a[h * S:(h + 1) * S, b, :, :, :].rearrange("p c j (g d) -> p c (j g) d", d=HD)
            return flat[:, :, h:h + 31:HPC + 2, :]

        def v_heads(b, h):
            return v_tok[h * S:(h + 1) * S, int(h != b), :].rearrange("p (c j g d) -> p c j g d", c=C, g=2, d=HD)[:, :, :, h, :]

        block = ctx.enter_context(nc.Block())
        NU = 3 * C + C

        @block.sync
        def _(sp):
            sp.dma_start(xt_raw[:], x_cols[0]).then_inc(xt_in, 16)
            for n in range(NU):
                if n >= RING_A:
                    sp.wait_ge(w_lo, n - RING_A + 1)
                src = w_qkv[n] if n < 3 * C else w_out[n - 3 * C]
                sp.dma_start(raw[:, n % RING_A, :], src).then_inc(raw_in[n % RING_A], 16)
                if n == 4:
                    sp.dma_start(lnp[:], ln_cols).then_inc(par_in, 16)
                    sp.dma_start(heads[:], head_rows).then_inc(par_in, 16)
                    sp.dma_start(bias[:], alibi_bias).then_inc(par_in, 16)
            sp.dma_start(x_tok[:].rearrange("p (t d) -> p t d", t=NT), x_rows).then_inc(x_in, 16)
            def swap_v(n):
                sp.wait_ge(clipped, 3 * n + 3)
                wait(sp, vblk_lo, n)
                for h in range(2):
                    sp.dma_start(v_tok[h * S:(h + 1) * S, 1, :],
                                 v_tok[(1 - h) * S:(2 - h) * S, 0, :]).then_inc(v_swapped, 16)

            swap_v(0)
            with sp.Fori(1, NT) as n:
                sp.wait_ge(xt_hi, n)
                sp.wait_ge(xt_lo, n)
                sp.dma_start(xt_raw[:], x_cols[n]).then_inc(xt_in, 16)
                swap_v(n)

        @block.tensor
        def _(pe):
            def qkv(n):
                pe.wait_ge(xt_hi, n + 1)
                pe.wait_ge(xt_lo, n + 1)
                for j in range(3):
                    wait(pe, clipped, 3 * n + max(j - 1, 0))
                    if isinstance(n, int):
                        pe.wait_ge(w_hi, C * (j + 1))
                        pe.wait_ge(w_lo, C * (j + 1))
                    for c in range(C):
                        last = products(nc, R[j % 2][:, :], [a[:, c, :] for a in xt],
                                        [a[:, C * j + c, :] for a in wqkv], start=(c == 0), stop=(c == C - 1))
                    last.then_inc(qkv_done, 1)

            def turn_qk(n):
                pe.wait_ge(qk_normed, n + 1)
                wait(pe, pt_lo, 4 * n - 4)
                for j in range(2):
                    for c in range(C):
                        last = nc.tensor.transpose(T[j][:, c * P:(c + 1) * P],
                                                   qk_tok[:, j, c * P:(c + 1) * P], ident[:])
                    last.then_inc(qkt_done, 1)

            def scores(i):
                pe.wait_ge(qz_hi, i + 1)
                pe.wait_ge(qz_lo, i + 1)
                pe.wait_ge(kblk_hi, i + 1)
                pe.wait_ge(kblk_lo, i + 1)
                for c in range(C):
                    wait(pe, masked, 4 * i + max(c - 1, 0))
                    for b in range(2):
                        last = products(nc, SC[c % 2][:, :], [a[:, c, b, :] for a in qz],
                                        [a[:, c, b, :, :] for a in kblk], start=(b == 0), stop=(b == 1))
                    last.then_inc(scores_done, 1)

            def values(i, n):
                def turn(c):
                    pe.wait_ge(probs_done, 2 * i + c // 2 + 1)
                    if c < 2:
                        if n is not None:
                            pe.wait_ge((q_affine, k_affine)[c], n + 1)
                    else:
                        pe.wait_ge(pt_lo, 4 * i + c - 1)
                    for j in range(HPC // 2):
                        h = HPC * c + 2 * j
                        last = nc.tensor.transpose(T[c % 2][:, j * P:(j + 1) * P], probs[:, h:h + 2, :],
                                                   ident[:])
                    last.then_inc(pt_done, 1)

                def weigh(c):
                    pe.wait_ge(pt_hi, 4 * i + c + 1)
                    pe.wait_ge(pt_lo, 4 * i + c + 1)
                    if c == 0:
                        pe.wait_ge(vblk_hi, i + 1)
                        pe.wait_ge(vblk_lo, i + 1)
                        wait(pe, ot_lo, i)
                    for b in range(2):
                        for j in range(HPC // 2):
                            last = products(nc, O[:, c * P + b * S:c * P + (b + 1) * S],
                                            [a[:, b, c, j, :] for a in vblk],
                                            [a[:, c % 2, j, b * S:(b + 1) * S] for a in pt],
                                            start=(j == 0), stop=(j == HPC // 2 - 1))
                    last.then_inc(pv_done, 1)

                turn(0)
                turn(1)
                for c in range(C):
                    weigh(c)
                    if c + 2 < C:
                        turn(c + 2)

            def project(i):
                pe.wait_ge(ot_hi, i + 1)
                pe.wait_ge(ot_lo, i + 1)
                wait(pe, y_added, i)
                for c in range(C):
                    last = products(nc, Y[:, :], [a[:, c, :] for a in ot], [a[:, c, :] for a in wout],
                                    start=(c == 0), stop=(c == C - 1))
                last.then_inc(y_done, 1)

            pe.wait_ge(ident_in, 1)
            qkv(0)
            turn_qk(0)
            pe.wait_ge(w_hi, NU)
            pe.wait_ge(w_lo, NU)

            def tile(i):
                scores(i)
                qkv(i + 1)
                turn_qk(i + 1)
                values(i, i + 1)
                project(i)

            tile(0)
            with pe.Fori(1, NT - 1) as i:
                tile(i)
            scores(NT - 1)
            values(NT - 1, None)
            project(NT - 1)

        @block.scalar
        def _(act):
            def split_x(n):
                act.wait_ge(xt_in, 16 * n + 16)
                wait(act, qkv_done, 3 * n)
                nc.scalar.activation(xt[0][:], xt_raw[:], ACT.Copy).then_inc(xt_hi, 1)

            def affine(n):
                for j, done in ((0, q_affine), (1, k_affine)):
                    act.wait_ge(qkt_done, 2 * n + j + 1)
                    wait(act, (qz_lo, k_split)[j], n)
                    for c in range(C):
                        last = nc.scalar.activation(qk_col[:, j, c, :], T[j][:, c * P:(c + 1) * P],
                                                    ACT.Identity, bias=lnp[:, 2 * j + 1, c:c + 1],
                                                    scale=lnp[:, 2 * j, c:c + 1])
                    last.then_inc(done, 1)

            def spread_q(n):
                wait(act, scores_done, 4 * n)
                act.wait_ge(q_affine, n + 1)
                for b in range(2):
                    last = nc.scalar.activation(qz[0][:, :, b, b * S:(b + 1) * S],
                                                qk_col[:, 0, :, b * S:(b + 1) * S], ACT.Copy)
                last.then_inc(qz_hi, 1)

            def spread_k(n):
                act.wait_ge(k_split, n + 1)
                wait(act, scores_done, 4 * n)
                for h in range(HPC):
                    last = nc.scalar.activation(kblk[1][:, :, :, h, :],
                                                qk_tok[:, 1, :].rearrange("p (c b t) -> p c b t", c=C, b=2),
                                                ACT.Copy, scale=heads[:, h:h + 1])
                last.then_inc(kblk_lo, 1)

            def spread_v(n):
                act.wait_ge(clipped, 3 * n + 3)
                act.wait_ge(v_swapped, 32 * n + 32)
                wait(act, pv_done, 4 * n)
                for b in range(2):
                    for h in range(2):
                        rows = slice(h * S, (h + 1) * S)
                        dst = vblk_diag(vblk[0], b, h)
                        last = nc.scalar.activation(dst, v_heads(b, h), ACT.Copy)
                last.then_inc(vblk_hi, 1)

            def exps(i):
                for f in range(2):
                    act.wait_ge(shifted, 2 * i + f + 1)
                    v = probs[:, f * NH // 2:(f + 1) * NH // 2, :]
                    nc.scalar.activation(v, v, ACT.Exp).then_inc(exp_done, 1)

            def probs_hi(i):
                for c in range(C):
                    act.wait_ge(pt_done, 4 * i + c + 1)
                    wait(act, pv_done, 4 * i + max(c - 1, 0))
                    nc.scalar.activation(pt[0][:, c % 2, :, :], T[c % 2][:, :], ACT.Copy).then_inc(pt_hi, 1)
                act.wait_ge(pv_done, 4 * i + 4)
                wait(act, y_done, i)
                nc.scalar.activation(ot[0][:], O[:, :], ACT.Copy).then_inc(ot_hi, 1)

            split_x(0)
            for n in range(NU):
                act.wait_ge(raw_in[n % RING_A], 16 * (n // RING_A) + 16)
                dst = wqkv[0][:, n, :] if n < 3 * C else wout[0][:, n - 3 * C, :]
                nc.scalar.activation(dst, raw[:, n % RING_A, :], ACT.Copy).then_inc(w_hi, 1)
            act.wait_ge(par_in, 48)
            act.wait_ge(zeroed, 4)
            affine(0)
            spread_q(0)
            spread_k(0)
            spread_v(0)

            def tile(i):
                split_x(i + 1)
                exps(i)
                affine(i + 1)
                spread_q(i + 1)
                probs_hi(i)
                spread_k(i + 1)
                spread_v(i + 1)

            tile(0)
            with act.Fori(1, NT - 1) as i:
                tile(i)
            exps(NT - 1)
            probs_hi(NT - 1)

        @block.vector
        def _(dve):
            def split_x(n):
                dve.wait_ge(xt_hi, n + 1)
                nc.vector.tensor_tensor(xt[1][:], xt_raw[:], xt[0][:].bitcast(F32), ALU.subtract).then_inc(xt_lo, 1)

            def clip(n, item, dst):
                dve.wait_ge(qkv_done, 3 * n + item + 1)
                nc.vector.tensor_scalar(dst, R[item % 2][:, :], CLIP, -CLIP, ALU.min, ALU.max).then_inc(clipped, 1)

            def clip_qk(n):
                wait(dve, qkt_done, 2 * n)
                wait(dve, kblk_lo, n)
                for j in range(2):
                    clip(n, j, qk_tok[:, j, :])

            def clip_v(n):
                wait(dve, vblk_hi, n)
                clip(n, 2, v_tok[:, 0, :])

            def norm_qk(n, chain):
                dve.wait_ge(clipped, 3 * n + 2)
                for j in range(2):
                    last = nc.vector.bn_stats(st6[:, j, :], qk_tok[:, j, :])
                chain.link(last)
                nc.vector.memset(tmp2[:], 0.0)
                for j in range(2):
                    last = nc.vector.bn_aggr(mv[:, j, :], st6[:, j, :])
                chain.link(last)
                rsqrt(nc, chain, mv[:, :, 1], rstd[:], tmp2[:])
                for j in range(2):
                    last = nc.vector.tensor_scalar(qk_tok[:, j, :], qk_tok[:, j, :], mv[:, j, 0:1], rstd[:, j:j + 1],
                                                   ALU.subtract, ALU.mult)
                last.then_inc(qk_normed, 1)

            def split_k(n):
                dve.wait_ge(k_affine, n + 1)
                hi, lo = [qk_tok[:, j, :] for j in range(2)]
                col = qk_col[:, 1, :, :].rearrange("p c t -> p (c t)")
                nc.vector.tensor_copy(hi.bitcast(F32R), col).then_inc(step_n, 1)
                dve.wait_ge(step_n, STEPS_N * n + STEPS_N)
                nc.vector.tensor_tensor(lo.bitcast(F32R), col, hi, ALU.subtract).then_inc(k_split, 1)

            def spread_k(n, hs):
                if 0 in hs:
                    wait(dve, scores_done, 4 * n)
                for h in hs:
                    last = nc.vector.tensor_scalar(kblk[0][:, :, :, h, :],
                                                   qk_tok[:, 0, :].rearrange("p (c b t) -> p c b t", c=C, b=2),
                                                   heads[:, h:h + 1], None, ALU.mult)
                if HPC - 1 in hs:
                    last.then_inc(kblk_hi, 1)

            def spread_q(n):
                dve.wait_ge(qz_hi, n + 1)
                for b in range(2):
                    cols = slice(b * S, (b + 1) * S)
                    last = nc.vector.tensor_tensor(qz[1][:, :, b, cols], qk_col[:, 0, :, cols],
                                                   qz[0][:, :, b, cols].bitcast(F32), ALU.subtract)
                last.then_inc(qz_lo, 1)

            def spread_v(n):
                dve.wait_ge(vblk_hi, n + 1)
                for b in range(2):
                    for h in range(2):
                        last = nc.vector.tensor_tensor(vblk_diag(vblk[1], b, h), v_heads(b, h),
                                                       vblk_diag(vblk[0], b, h).bitcast(F32), ALU.subtract)
                last.then_inc(vblk_lo, 1)

            def mask(i):
                wait(dve, pt_done, 4 * i)
                for c in range(C):
                    dve.wait_ge(scores_done, 4 * i + c + 1)
                    hs = slice(HPC * c, HPC * (c + 1))
                    nc.vector.scalar_tensor_tensor(probs[:, hs, :], SC[c % 2][:, :].rearrange("p (h k) -> p h k", k=S),
                                                   HD ** -0.5, bias[:, hs, :], ALU.mult, ALU.add).then_inc(masked, 1)
                    if c % 2 == 1:
                        f = c // 2
                        hf = slice(f * NH // 2, (f + 1) * NH // 2)
                        dve.wait_ge(masked, 4 * i + c + 1)
                        nc.vector.tensor_reduce(mx[:, hf], probs[:, hf, :], AX.X, ALU.max).then_inc(row_max, 1)

            def invert(i, chain):
                for f in range(2):
                    hf = slice(f * NH // 2, (f + 1) * NH // 2)
                    dve.wait_ge(exp_done, 2 * i + f + 1)
                    chain.link(nc.vector.tensor_reduce(den[:, hf], probs[:, hf, :], AX.X, ALU.add))
                    nc.vector.reciprocal(den[:, hf], den[:, hf]).then_inc(inverse, 1)

            def probs_lo(i, cs):
                for c in cs:
                    dve.wait_ge(pt_hi, 4 * i + c + 1)
                    nc.vector.tensor_tensor(pt[1][:, c % 2, :, :].rearrange("p j t -> p (j t)"), T[c % 2][:, :],
                                            pt[0][:, c % 2, :, :].rearrange("p j t -> p (j t)").bitcast(F32),
                                            ALU.subtract).then_inc(pt_lo, 1)

            def finish(i):
                dve.wait_ge(ot_hi, i + 1)
                nc.vector.tensor_tensor(ot[1][:].rearrange("p c t -> p (c t)"), O[:, :],
                                        ot[0][:].rearrange("p c t -> p (c t)").bitcast(F32),
                                        ALU.subtract).then_inc(ot_lo, 1)
                dve.wait_ge(y_done, i + 1)
                rows = x_tok[:, bass.ds(i * D, D)]
                nc.vector.tensor_tensor(rows, Y[:, :], rows, ALU.add).then_inc(y_added, 1)

            STEPS_N = 2 + RSQRT_OPS + 1

            def chain_n(n):
                return Chain(dve, step_n, STEPS_N * n)

            split_x(0)
            for n in range(NU):
                dve.wait_ge(w_hi, n + 1)
                w, k = (wqkv, n) if n < 3 * C else (wout, n - 3 * C)
                nc.vector.tensor_tensor(w[1][:, k, :], raw[:, n % RING_A, :], w[0][:, k, :].bitcast(F32),
                                        ALU.subtract).then_inc(w_lo, 1)
            clip_qk(0)
            clip_v(0)
            norm_qk(0, chain_n(0))
            dve.wait_ge(par_in, 48)
            split_k(0)
            dve.wait_ge(k_split, 1)
            dve.wait_ge(zeroed, 4)
            spread_k(0, range(HPC))
            spread_q(0)
            spread_v(0)
            dve.wait_ge(x_in, 16)

            def tile(i):
                n = i + 1
                split_x(n)
                mask(i)
                clip_qk(n)
                invert(i, Chain(dve, step_i, 2 * i))
                clip_v(n)
                norm_qk(n, chain_n(n))
                probs_lo(i, [0, 1])
                split_k(n)
                dve.wait_ge(k_split, n + 1)
                spread_k(n, range(4))
                probs_lo(i, [2])
                spread_k(n, range(4, 6))
                probs_lo(i, [3])
                spread_k(n, range(6, 8))
                spread_q(n)
                finish(i)
                spread_v(n)

            tile(0)
            with dve.Fori(1, NT - 1) as i:
                tile(i)
            i = NT - 1
            mask(i)
            invert(i, Chain(dve, step_i, 2 * i))
            probs_lo(i, range(4))
            finish(i)

        @block.gpsimd
        def _(pool):
            nc.gpsimd.memset(ident[:], 0.0).then_inc(ident_z, 1)
            pool.wait_ge(ident_z, 1)
            nc.gpsimd.affine_select(out=ident[:], in_=ident[:], compare_op=ALU.not_equal, fill=1.0, base=0,
                                    pattern=[[-1, P]], channel_multiplier=1).then_inc(ident_in, 1)
            for a in (qz[0], qz[1], vblk[0], vblk[1]):
                nc.gpsimd.memset(a[:].bitcast(F32), 0.0).then_inc(zeroed, 1)

            def softmax(i):
                for f in range(2):
                    hf = slice(f * NH // 2, (f + 1) * NH // 2)
                    v = probs[:, hf, :]
                    pool.wait_ge(row_max, 2 * i + f + 1)
                    nc.gpsimd.tensor_tensor(v, v, mx[:, hf].unsqueeze(2).broadcast_to([P, NH // 2, S]),
                                            ALU.subtract).then_inc(shifted, 1)
                for f in range(2):
                    hf = slice(f * NH // 2, (f + 1) * NH // 2)
                    v = probs[:, hf, :]
                    pool.wait_ge(inverse, 2 * i + f + 1)
                    nc.gpsimd.tensor_tensor(v, v, den[:, hf].unsqueeze(2).broadcast_to([P, NH // 2, S]),
                                            ALU.mult).then_inc(probs_done, 1)

            softmax(0)
            with pool.Fori(1, NT) as i:
                softmax(i)


class NormTurn:

    def __init__(self, nc, ctx, name, top, xt, banks):
        self.nc, self.x_tok, self.ident, self.xt, self.banks = nc, top["x_tok"], top["ident"], xt, banks

        def sb(part, shape):
            return ctx.enter_context(nc.sbuf_tensor(name + part, shape, F32))

        self.st6, self.mv = sb("_st6", [P, NT, 6]), sb("_mv", [P, NT, 2])
        self.rstd, self.tmp = sb("_rstd", [P, NT]), sb("_tmp", [P, NT])
        self.step, self.normed, self.turned, self.hi, self.lo = [
            ctx.enter_context(nc.semaphore(name + part)) for part in ("_step", "_normed", "_turned", "_hi", "_lo")]

    def row(self, t):
        return self.x_tok[:, t * D:(t + 1) * D]

    def norm(self, dve):
        nc, chain = self.nc, Chain(dve, self.step, 0)
        for t in range(NT):
            last = nc.vector.bn_stats(self.st6[:, t, :], self.row(t))
        chain.link(last)
        for t in range(NT):
            last = nc.vector.bn_aggr(self.mv[:, t, :], self.st6[:, t, :])
        chain.link(last)
        rsqrt(nc, chain, self.mv[:, :, 1], self.rstd[:], self.tmp[:])
        for t in range(NT):
            nc.vector.tensor_scalar(self.row(t), self.row(t), self.mv[:, t, 0:1], self.rstd[:, t:t + 1],
                                    ALU.subtract, ALU.mult).then_inc(self.normed, 1)

    def turn(self, pe):
        for t in range(NT):
            pe.wait_ge(self.normed, t + 1)
            wait(pe, self.lo, t - len(self.banks) + 1)
            for c in range(C):
                last = self.nc.tensor.transpose(self.banks[t % len(self.banks)][:, c * P:(c + 1) * P],
                                                self.row(t)[:, c * P:(c + 1) * P], self.ident[:])
            last.then_inc(self.turned, 1)

    def bank(self, t):
        return self.banks[t % len(self.banks)][:, :].rearrange("p (c t) -> p c t", c=C)

    def split_hi(self, act):
        for t in range(NT):
            act.wait_ge(self.turned, t + 1)
            self.nc.scalar.activation(self.xt[0][:, :, t * P:(t + 1) * P], self.bank(t), ACT.Copy).then_inc(self.hi, 1)

    def split_lo(self, dve):
        for t in range(NT):
            dve.wait_ge(self.hi, t + 1)
            self.nc.vector.tensor_tensor(self.xt[1][:, :, t * P:(t + 1) * P], self.bank(t),
                                         self.xt[0][:, :, t * P:(t + 1) * P].bitcast(F32),
                                         ALU.subtract).then_inc(self.lo, 1)


def cross_attention(nc, top, xt, ctx_cols, w_q, w_kv, w_d, causal_bias):
    with ExitStack() as ctx:
        def sb(name, shape, dt=F32):
            return ctx.enter_context(nc.sbuf_tensor(name, shape, dt))

        def split(name, shape):
            return sb(name + "_hi", shape, F32R), sb(name + "_lo", shape, F32R)

        def sem(name):
            return ctx.enter_context(nc.semaphore(name))

        x_tok, ident = top["x_tok"], top["ident"]
        raw = sb("c_raw", [P, RING, D])
        ctx_raw = sb("ctx_raw", [P, 2, D])
        ct = split("ct", [P, C, TOK])
        wq = split("wq", [P, HG, C, DK])
        wkv = split("wkv", [P, 2, C, DK])
        wd = split("wd", [P, HG, D])
        q = split("q", [P, 2 * TH, HG, S])
        k = split("k", [P, HALF])
        v = split("v", [P, 2, TH, DK])
        v_cols = sb("v_cols", [P, HALF])
        st = sb("scores_t", [P, TH, HG * S])
        probs = sb("c_probs", [P, TH, 2, 2, S])
        pt = split("c_pt", [P, 2, 2, HG * S])
        ot = split("c_ot", [P, HG, HALF])
        mask = sb("causal", [P, S])
        mx = sb("c_mx", [P, 4 * TH])
        den = sb("c_den", [P, 4 * TH])

        def ps(name):
            return ctx.enter_context(nc.psum_tensor(name, [P, D], F32))

        R = [ps("cR0"), ps("cR1")]
        SC = [ps("cS0"), ps("cS1")]
        T = [ps("cT0"), ps("cT1")]
        O = [ps("cO0"), ps("cO1")]
        nt = NormTurn(nc, ctx, "ln1", top, xt, SC + T)

        raw_in = [sem(f"c_raw_in{i}") for i in range(RING)]
        ctx_in = [sem("ctx_in0"), sem("ctx_in1")]
        mask_in = sem("mask_in")
        ct_hi, ct_lo = sem("ct_hi"), sem("ct_lo")
        w_hi, w_lo = sem("c_w_hi"), sem("c_w_lo")
        q_done, k_done, v_done, y_done = sem("q_done"), sem("k_done"), sem("v_done"), sem("c_y_done")
        q_hi, k_hi, v_hi = sem("q_hi"), sem("k_hi"), sem("v_hi")
        q_lo, k_lo, v_lo, y_added = sem("q_lo"), sem("k_lo"), sem("v_lo"), sem("c_y_added")
        vt_out, vt_done = sem("vt_out"), sem("vt_done")
        keyed, st_out = sem("c_keyed"), sem("c_st_out")
        scores_done, masked, row_max = sem("c_scores_done"), sem("c_masked"), sem("c_row_max")
        shifted, exp_done, summed = sem("c_shifted"), sem("c_exp_done"), sem("c_summed")
        inverse, probs_done = sem("c_inverse"), sem("c_probs_done")
        pt_done, pt_hi, pt_lo = sem("c_pt_done"), sem("c_pt_hi"), sem("c_pt_lo")
        pv_done, o_hi, o_lo = sem("c_pv_done"), sem("c_o_hi"), sem("c_o_lo")

        FIRST, PER = HG + 2, 2 * HG + 2

        def unit(g, j):
            return j if g is None else FIRST + PER * g + j

        def slot(j):
            return (FIRST + j) % RING, (FIRST + j) // RING

        def out_cols(a, u, b):
            return a[:].rearrange("p h (t b s) -> p t h b s", t=TH, b=2)[:, 2 * u:2 * u + 2, :, b, :]

        block = ctx.enter_context(nc.Block())

        @block.sync
        def _(sp):
            for n in range(2 * C):
                if n >= 2:
                    sp.wait_ge(ct_lo, n - 1)
                sp.dma_start(ctx_raw[:, n % 2, :], ctx_cols[n // 2, n % 2]).then_inc(ctx_in[n % 2], 16)
                if n == 1:
                    sp.dma_start(mask[:], causal_bias).then_inc(mask_in, 16)
                if n < FIRST:
                    if n >= RING:
                        sp.wait_ge(w_lo, n - RING + 1)
                    src = w_q[0, n] if n < HG else w_kv[0, n - HG]
                    sp.dma_start(raw[:, n % RING, :], src).then_inc(raw_in[n % RING], 16)

            def stream(g):
                for j in range(PER):
                    if j >= HG and isinstance(g, int) and g == G - 1:
                        return
                    sp.wait_ge(w_lo, unit(g, j) - RING + 1)
                    src = w_d[g, j] if j < HG else w_q[g + 1, j - HG] if j < 2 * HG else w_kv[g + 1, j - 2 * HG]
                    sp.dma_start(raw[:, slot(j)[0], :], src).then_inc(raw_in[slot(j)[0]], 16)

            stream(0)
            with sp.Fori(1, G - 1) as g:
                stream(g)
            stream(G - 1)

        @block.tensor
        def _(pe):
            def project_q(p, g, hf):
                for h in range(HG):
                    pe.wait_ge(w_lo, PER * g + h + 1)
                    if h < 2:
                        if isinstance(p, int) and p == 1:
                            pe.wait_ge((k_lo, v_lo)[h], 1)
                        else:
                            wait(pe, y_added, 4 * p - 5 + h)
                    else:
                        pe.wait_ge(q_lo, 4 * p + h - 1)
                    for c in range(C):
                        last = products(nc, R[h % 2][:, :], [a[:, h, c, :] for a in wq],
                                        [a[:, c, hf * HALF:(hf + 1) * HALF] for a in xt],
                                        start=(c == 0), stop=(c == C - 1))
                    last.then_inc(q_done, 1)

            def project_k(p, g, hf):
                pe.wait_ge(w_lo, PER * g + HG + 1)
                pe.wait_ge(q_lo, 4 * p + 3)
                for c in range(C):
                    last = products(nc, R[0][:, :], [a[:, 0, c, :] for a in wkv],
                                    [a[:, c, hf * HALF:(hf + 1) * HALF] for a in ct],
                                    start=(c == 0), stop=(c == C - 1))
                last.then_inc(k_done, 1)

            def project_v(p, g, hf):
                pe.wait_ge(w_lo, PER * g + HG + 2)
                pe.wait_ge(q_lo, 4 * p + 4)
                for c in range(C):
                    last = products(nc, R[1][:, :], [a[:, 1, c, :] for a in wkv],
                                    [a[:, c, hf * HALF:(hf + 1) * HALF] for a in ct],
                                    start=(c == 0), stop=(c == C - 1))
                last.then_inc(v_done, 1)

            def turn_v(p):
                pe.wait_ge(vt_out, p + 1)
                for t in range(TH):
                    last = nc.tensor.transpose(R[1][:, t * DK:(t + 1) * DK], v_cols[:, t * P:(t + 1) * P], ident[:])
                last.then_inc(vt_done, 1)

            def scores(s):
                pe.wait_ge(q_lo, 4 * s + 4)
                pe.wait_ge(k_lo, s + 1)
                for t in range(TH):
                    wait(pe, st_out, 4 * s + t - 1)
                    last = products(nc, SC[t % 2][:, :], [a[:, t * P:(t + 1) * P] for a in k],
                                    [a[:, 2 * t:2 * t + 2, :, :] for a in q])
                    last.then_inc(keyed, 1)

            def turn_scores(s):
                wait(pe, pt_lo, 2 * s)
                for u in range(2):
                    pe.wait_ge(st_out, 4 * s + 2 * u + 2)
                    for t in (2 * u, 2 * u + 1):
                        for r in range(2):
                            col = (t % 2) * 256 + r * 128
                            last = nc.tensor.transpose(T[u][:, col:col + P], st[:, t, r * P:(r + 1) * P], ident[:])
                    last.then_inc(scores_done, 1)

            def turn(s):
                pe.wait_ge(probs_done, s + 1)
                for u in range(2):
                    for t in (2 * u, 2 * u + 1):
                        for r in range(2):
                            col = (t % 2) * 256 + r * 128
                            last = nc.tensor.transpose(T[u][:, col:col + P], probs[:, t, r, :, :], ident[:])
                    last.then_inc(pt_done, 1)

            def weigh(s, u, par):
                pe.wait_ge(pt_lo, 2 * s + u + 1)
                pe.wait_ge(v_lo, s + 1)
                wait(pe, o_lo, 2 * s + u)
                for t in range(2):
                    for i, (lv, lp) in enumerate(((1, 0), (0, 1), (0, 0))):
                        for b in range(2):
                            rows = slice(b * S, (b + 1) * S)
                            last = nc.tensor.matmul(O[b][:, t * 256:(t + 1) * 256], v[lv][rows, par, 2 * u + t, :],
                                                    pt[lp][rows, u, t, :], start=(i == 0), stop=(i == 2))
                last.then_inc(pv_done, 1)

            def project_out(s, g, more):
                pe.wait_ge(w_lo, PER * g + PER)
                pe.wait_ge(o_lo, 2 * s + 2)
                for t in range(TH):
                    if t < 2 and more:
                        pe.wait_ge((k_lo, v_lo)[t], s + 2)
                    else:
                        pe.wait_ge(y_added, 4 * s + t - 1)
                    for h in range(HG):
                        last = products(nc, R[t % 2][:, :], [a[:, h, t * P:(t + 1) * P] for a in ot],
                                        [a[:, h, :] for a in wd], start=(h == 0), stop=(h == HG - 1))
                    last.then_inc(y_done, 1)
                    if t == 0 and more:
                        turn_scores(s + 1)

            def step(s, g, hf, more=True):
                g1, hf1 = (g, 1) if hf == 0 else (g + 1, 0)
                if more:
                    project_q(s + 1, g1, hf1)
                turn(s)
                if more:
                    project_k(s + 1, g1, hf1)
                weigh(s, 0, hf)
                if more:
                    project_v(s + 1, g1, hf1)
                weigh(s, 1, hf)
                if more:
                    scores(s + 1)
                    turn_v(s + 1)
                project_out(s, g, more)

            nt.turn(pe)
            pe.wait_ge(nt.lo, NT)
            pe.wait_ge(ct_lo, 2 * C)
            project_q(0, 0, 0)
            project_k(0, 0, 0)
            project_v(0, 0, 0)
            scores(0)
            turn_v(0)
            turn_scores(0)
            step(0, 0, 0)
            step(1, 0, 1)
            with pe.Fori(1, G - 1) as g:
                step(2 * g, g, 0)
                step(2 * g + 1, g, 1)
            step(2 * G - 2, G - 1, 0)
            step(2 * G - 1, G - 1, 1, more=False)

        @block.scalar
        def _(act):
            def weights_hi(g, js):
                for j in js:
                    if g is None:
                        act.wait_ge(raw_in[j % RING], 16 * (j // RING) + 16)
                        src = raw[:, j % RING, :]
                        dst = wq[0][:, j, :, :] if j < HG else wkv[0][:, j - HG, :, :]
                        dst = dst.rearrange("p c d -> p (c d)")
                    else:
                        n, use = slot(j)
                        act.wait_ge(raw_in[n], 16 * (2 * g + use) + 16)
                        src = raw[:, n, :]
                        if j < HG:
                            wait(act, y_done, 8 * g)
                            dst = wd[0][:, j, :]
                        elif j < 2 * HG:
                            act.wait_ge(q_done, 8 * g + 8)
                            dst = wq[0][:, j - HG, :, :].rearrange("p c d -> p (c d)")
                        else:
                            act.wait_ge(k_done if j == 2 * HG else v_done, 2 * g + 2)
                            dst = wkv[0][:, j - 2 * HG, :, :].rearrange("p c d -> p (c d)")
                    nc.scalar.activation(dst, src, ACT.Copy).then_inc(w_hi, 1)

            def q_split(p):
                for h in range(HG):
                    act.wait_ge(q_done, 4 * p + h + 1)
                    wait(act, keyed, 4 * p)
                    nc.scalar.activation(q[0][:, :, h, :], R[h % 2][:, :].rearrange("p (t s) -> p t s", s=S),
                                         ACT.Copy).then_inc(q_hi, 1)

            def k_split(p):
                act.wait_ge(k_done, p + 1)
                wait(act, keyed, 4 * p)
                nc.scalar.activation(k[0][:], R[0][:, :], ACT.Copy).then_inc(k_hi, 1)

            def v_split(p, par):
                act.wait_ge(vt_done, p + 1)
                wait(act, pv_done, 2 * (p - 1))
                nc.scalar.activation(v[0][:, par, :, :], R[1][:, :], ACT.Copy).then_inc(v_hi, 1)

            def v_out(p):
                act.wait_ge(v_done, p + 1)
                wait(act, vt_done, p)
                nc.scalar.activation(v_cols[:], R[1][:, :], ACT.Copy).then_inc(vt_out, 1)

            def scores_out(s):
                wait(act, scores_done, 2 * s)
                for t in range(TH):
                    act.wait_ge(keyed, 4 * s + t + 1)
                    for b in range(2):
                        rows = slice(b * S, (b + 1) * S)
                        last = nc.scalar.activation(st[rows, t, :], SC[t % 2][rows, b * 256:(b + 1) * 256], ACT.Copy)
                    last.then_inc(st_out, 1)

            def exps(s):
                act.wait_ge(shifted, s + 1)
                nc.scalar.activation(probs[:], probs[:], ACT.Exp).then_inc(exp_done, 1)

            def probs_split(s):
                wait(act, pv_done, 2 * s)
                for u in range(2):
                    act.wait_ge(pt_done, 2 * s + u + 1)
                    nc.scalar.activation(pt[0][:, u, :, :], T[u][:, :], ACT.Copy).then_inc(pt_hi, 1)

            def out_split(s, u):
                act.wait_ge(pv_done, 2 * s + u + 1)
                wait(act, y_done, 4 * s)
                for b in range(2):
                    last = nc.scalar.activation(out_cols(ot[0], u, b),
                                                O[b][:, :].rearrange("p (t h s) -> p t h s", t=2, h=HG), ACT.Copy)
                last.then_inc(o_hi, 1)

            def step(s, g, hf, more=True):
                exps(s)
                if hf == 0:
                    weights_hi(g, range(HG))
                if more:
                    q_split(s + 1)
                probs_split(s)
                if more:
                    k_split(s + 1)
                out_split(s, 0)
                if more:
                    v_out(s + 1)
                out_split(s, 1)
                if more:
                    scores_out(s + 1)
                    v_split(s + 1, 1 - hf)
                if hf == 0 and not (isinstance(g, int) and g == G - 1):
                    weights_hi(g, range(HG, PER))

            for n in range(2 * C):
                act.wait_ge(ctx_in[n % 2], 16 * (n // 2) + 16)
                nc.scalar.activation(ct[0][:, n // 2, (n % 2) * D:(n % 2 + 1) * D], ctx_raw[:, n % 2, :],
                                     ACT.Copy).then_inc(ct_hi, 1)
                if n < FIRST:
                    weights_hi(None, [n])
            nt.split_hi(act)
            q_split(0)
            k_split(0)
            v_out(0)
            scores_out(0)
            v_split(0, 0)
            step(0, 0, 0)
            step(1, 0, 1)
            with act.Fori(1, G - 1) as g:
                step(2 * g, g, 0)
                step(2 * g + 1, g, 1)
            step(2 * G - 2, G - 1, 0)
            step(2 * G - 1, G - 1, 1, more=False)

        @block.vector
        def _(dve):
            def lo(dst, src, hi, done):
                return nc.vector.tensor_tensor(dst, src, hi.bitcast(F32), ALU.subtract).then_inc(done, 1)

            def q_split(p):
                for h in range(HG):
                    dve.wait_ge(q_hi, 4 * p + h + 1)
                    lo(q[1][:, :, h, :], R[h % 2][:, :].rearrange("p (t s) -> p t s", s=S), q[0][:, :, h, :], q_lo)

            def k_split(p):
                dve.wait_ge(k_hi, p + 1)
                lo(k[1][:], R[0][:, :], k[0][:], k_lo)

            def v_split(p, par):
                dve.wait_ge(v_hi, p + 1)
                lo(v[1][:, par, :, :].rearrange("p t d -> p (t d)"), R[1][:, :],
                   v[0][:, par, :, :].rearrange("p t d -> p (t d)"), v_lo)

            def probs_split(s):
                for u in range(2):
                    dve.wait_ge(pt_hi, 2 * s + u + 1)
                    lo(pt[1][:, u, :, :].rearrange("p t c -> p (t c)"), T[u][:, :],
                       pt[0][:, u, :, :].rearrange("p t c -> p (t c)"), pt_lo)

            def out_split(s, u):
                dve.wait_ge(o_hi, 2 * s + u + 1)
                for b in range(2):
                    last = nc.vector.tensor_tensor(out_cols(ot[1], u, b),
                                                   O[b][:, :].rearrange("p (t h s) -> p t h s", t=2, h=HG),
                                                   out_cols(ot[0], u, b).bitcast(F32), ALU.subtract)
                last.then_inc(o_lo, 1)

            def mask_scores(s):
                wait(dve, pt_done, 2 * s)
                for u in range(2):
                    dve.wait_ge(scores_done, 2 * s + u + 1)
                    rows = probs[:, 2 * u:2 * u + 2, :, :, :].rearrange("p t r b k -> p (t r b) k")
                    nc.vector.scalar_tensor_tensor(rows, T[u][:, :].rearrange("p (n k) -> p n k", k=S), DK ** -0.5,
                                                   mask[:].unsqueeze(1).broadcast_to([P, 2 * HG, S]),
                                                   ALU.mult, ALU.add).then_inc(masked, 1)
                dve.wait_ge(masked, 2 * s + 2)
                nc.vector.tensor_reduce(mx[:], probs[:].rearrange("p t r b k -> p (t r b) k"), AX.X,
                                        ALU.max).then_inc(row_max, 1)

            def invert(s):
                dve.wait_ge(exp_done, s + 1)
                nc.vector.tensor_reduce(den[:], probs[:].rearrange("p t r b k -> p (t r b) k"), AX.X,
                                        ALU.add).then_inc(summed, 1)
                dve.wait_ge(summed, s + 1)
                nc.vector.reciprocal(den[:], den[:]).then_inc(inverse, 1)

            def add_out(s, hf, ts):
                for t in ts:
                    dve.wait_ge(y_done, 4 * s + t + 1)
                    row = nt.row(hf * TH + t)
                    nc.vector.tensor_tensor(row, R[t % 2][:, :], row, ALU.add).then_inc(y_added, 1)

            def step(s, hf, first=False, more=True):
                mask_scores(s)
                if not first:
                    add_out(s - 1, 1 - hf, (0, 1))
                invert(s)
                if not first:
                    add_out(s - 1, 1 - hf, (2, 3))
                if more:
                    q_split(s + 1)
                probs_split(s)
                if more:
                    k_split(s + 1)
                out_split(s, 0)
                out_split(s, 1)
                if more:
                    v_split(s + 1, 1 - hf)

            nt.norm(dve)
            nt.split_lo(dve)
            q_split(0)
            k_split(0)
            v_split(0, 0)
            dve.wait_ge(mask_in, 16)
            step(0, 0, first=True)
            step(1, 1)
            with dve.Fori(1, G - 1) as g:
                step(2 * g, 0)
                step(2 * g + 1, 1)
            step(2 * G - 2, 0)
            step(2 * G - 1, 1, more=False)
            add_out(2 * G - 1, 1, range(TH))

        @block.gpsimd
        def _(pool):
            def weights_lo(g, js):
                for j in js:
                    pool.wait_ge(w_hi, unit(g, j) + 1)
                    if g is None:
                        n, w, at = j % RING, wq if j < HG else wkv, j if j < HG else j - HG
                    else:
                        n = slot(j)[0]
                        w, at = (wd, j) if j < HG else (wq, j - HG) if j < 2 * HG else (wkv, j - 2 * HG)
                    if w is wd:
                        dst, hi = w[1][:, at, :], w[0][:, at, :]
                    else:
                        dst, hi = [w[m][:, at, :, :].rearrange("p c d -> p (c d)") for m in (1, 0)]
                    nc.gpsimd.tensor_tensor(dst, raw[:, n, :], hi.bitcast(F32), ALU.subtract).then_inc(w_lo, 1)

            def softmax(s):
                v2 = probs[:].rearrange("p t r b k -> p (t r b) k")
                pool.wait_ge(row_max, s + 1)
                nc.gpsimd.tensor_tensor(v2, v2, mx[:].unsqueeze(2).broadcast_to([P, 4 * TH, S]),
                                        ALU.subtract).then_inc(shifted, 1)
                pool.wait_ge(inverse, s + 1)
                nc.gpsimd.tensor_tensor(v2, v2, den[:].unsqueeze(2).broadcast_to([P, 4 * TH, S]),
                                        ALU.mult).then_inc(probs_done, 1)

            def step(s, g, hf):
                softmax(s)
                last = isinstance(g, int) and g == G - 1
                if hf == 0:
                    weights_lo(g, range(HG if last else 2 * HG))
                elif not last:
                    weights_lo(g, range(2 * HG, PER))

            for n in range(2 * C):
                pool.wait_ge(ct_hi, n + 1)
                at = slice((n % 2) * D, (n % 2 + 1) * D)
                nc.gpsimd.tensor_tensor(ct[1][:, n // 2, at], ctx_raw[:, n % 2, :], ct[0][:, n // 2, at].bitcast(F32),
                                        ALU.subtract).then_inc(ct_lo, 1)
                if n < FIRST:
                    weights_lo(None, [n])
            step(0, 0, 0)
            step(1, 0, 1)
            with pool.Fori(1, G - 1) as g:
                step(2 * g, g, 0)
                step(2 * g + 1, g, 1)
            step(2 * G - 2, G - 1, 0)
            step(2 * G - 1, G - 1, 1)


def experts(nc, top, xt, w_gate, b_gate, w_e, b_e, before, out):
    with ExitStack() as ctx:
        def sb(name, shape, dt=F32):
            return ctx.enter_context(nc.sbuf_tensor(name, shape, dt))

        def split(name, shape):
            return sb(name + "_hi", shape, F32R), sb(name + "_lo", shape, F32R)

        def sem(name):
            return ctx.enter_context(nc.semaphore(name))

        x_tok = top["x_tok"]
        raw = sb("e_raw", [P, 2, C, D])
        we = split("we", [P, 2, C, D])
        wg_raw = sb("wg_raw", [P, C, E])
        wg = split("wg", [P, C, E])
        bg = sb("bg", [P, E])
        be = sb("be", [P, E * D])
        pred = sb("pred", [P, E, E])
        logits = sb("logits", [P, NT, E])
        beats = sb("beats", [P, NT, E, E])
        ties = sb("ties", [P, NT, E, E])
        rank = sb("rank", [P, NT, E])
        share = sb("share", [P, E * NT])
        cur = sb("cur", [P, 2, NT])
        gate = sb("gate", [E, TOK])
        pre = sb("pre", [P, 4, D])
        act_out = sb("act_out", [P, 4, D])
        st6 = sb("e_st6", [P, NT, 6])
        mv = sb("e_mv", [P, NT, 2])
        rstd = sb("e_rstd", [P, NT])
        tmp = sb("e_tmp", [P, NT])

        def ps(name):
            return ctx.enter_context(nc.psum_tensor(name, [P, D], F32))

        F = [ps(f"eF{i}") for i in range(4)]
        T = [ps("eT0"), ps("eT1")]
        GT = ps("eG")
        nt = NormTurn(nc, ctx, "ln2", top, xt, T)

        we_in = [sem("we_in0"), sem("we_in1")]
        g_in, be_in = sem("g_in"), sem("be_in")
        we_hi, we_lo = sem("we_hi"), sem("we_lo")
        wg_hi, wg_lo = sem("wg_hi"), sem("wg_lo")
        gate_cols, gate_out, gate_done, chosen = sem("gate_cols"), sem("gate_out"), sem("gate_done"), sem("chosen")
        item_done, biased, relu_done, added = sem("item_done"), sem("biased"), sem("relu_done"), sem("added")
        picked = sem("picked")
        step_d = sem("step_d")
        row_done, row_out = sem("row_done"), sem("row_out")

        block = ctx.enter_context(nc.Block())

        @block.sync
        def _(sp):
            def load(e, par):
                wait(sp, we_lo, C * (e - 1))
                sp.dma_start(raw[:, par, :, :], w_e[e].rearrange("c p h -> p c h")).then_inc(we_in[par], 16)

            load(0, 0)
            load(1, 1)
            sp.dma_start(wg_raw[:], w_gate).then_inc(g_in, 16)
            sp.dma_start(bg[:], b_gate.to_broadcast([P, E])).then_inc(g_in, 16)
            sp.dma_start(pred[:], before).then_inc(g_in, 16)
            sp.dma_start(be[:], b_e.to_broadcast([P, E * D])).then_inc(be_in, 16)
            with sp.Fori(1, E // 2) as n:
                load(2 * n, 0)
                load(2 * n + 1, 1)
            for t in range(NT):
                sp.wait_ge(row_done, t + 1)
                sp.dma_start(out[t], x_tok[:, t * D:(t + 1) * D]).then_inc(row_out, 16)
            sp.wait_ge(row_out, 16 * NT)

        @block.tensor
        def _(pe):
            nt.turn(pe)
            pe.wait_ge(nt.lo, NT)
            pe.wait_ge(wg_lo, 1)
            for hf in range(2):
                for c in range(C):
                    last = products(nc, F[2 + hf][0:E, :], [a[:, c, :] for a in wg],
                                    [a[:, c, hf * HALF:(hf + 1) * HALF] for a in xt],
                                    start=(c == 0), stop=(c == C - 1))
            last.then_inc(gate_cols, 1)

            def turn_gate():
                pe.wait_ge(gate_out, 1)
                for t in range(NT):
                    last = nc.tensor.transpose(GT[:, t * E:(t + 1) * E], gate[:, t * P:(t + 1) * P], top["ident"][0:E, 0:E])
                last.then_inc(gate_done, 1)

            def expert(e, par):
                pe.wait_ge(we_lo, C * (e + 1))
                for t in range(NT):
                    if isinstance(e, int) and e == 0 and t == 2:
                        turn_gate()
                    wait(pe, biased, NT * e + t - 3)
                    for c in range(C):
                        last = products(nc, F[t % 4][:, :], [a[:, c, t * P:(t + 1) * P] for a in xt],
                                        [a[:, par, c, :] for a in we], start=(c == 0), stop=(c == C - 1))
                    last.then_inc(item_done, 1)

            expert(0, 0)
            expert(1, 1)
            with pe.Fori(1, E // 2) as n:
                expert(2 * n, 0)
                expert(2 * n + 1, 1)

        @block.scalar
        def _(act):
            def weights_hi(n, par):
                act.wait_ge(we_in[par], 16 * n + 16)
                wait(act, item_done, NT * (2 * n + par - 1))
                for c in range(C):
                    nc.scalar.activation(we[0][:, par, c, :], raw[:, par, c, :], ACT.Copy).then_inc(we_hi, 1)

            def relus(e, par):
                for t in range(NT):
                    act.wait_ge(biased, NT * e + t + 1)
                    if t == 0:
                        act.wait_ge(picked, e + 1)
                    wait(act, added, NT * e + t - 3)
                    nc.scalar.activation(act_out[:, t % 4, :], pre[:, t % 4, :], ACT.Relu,
                                         scale=cur[:, par, t:t + 1]).then_inc(relu_done, 1)

            act.wait_ge(g_in, 48)
            nc.scalar.activation(wg[0][:], wg_raw[:], ACT.Copy).then_inc(wg_hi, 1)
            weights_hi(0, 0)
            weights_hi(0, 1)
            nt.split_hi(act)

            act.wait_ge(gate_cols, 1)
            for hf in range(2):
                last = nc.scalar.activation(gate[:, hf * HALF:(hf + 1) * HALF], F[2 + hf][0:E, :], ACT.Copy)
            last.then_inc(gate_out, 1)

            def pair(n, load=True):
                relus(2 * n, 0)
                if load:
                    weights_hi(n + 1, 0)
                relus(2 * n + 1, 1)
                if load:
                    weights_hi(n + 1, 1)

            pair(0)
            with act.Fori(1, E // 2 - 1) as n:
                pair(n)
            pair(E // 2 - 1, load=False)

        @block.vector
        def _(dve):
            nt.norm(dve)
            dve.wait_ge(wg_hi, 1)
            nc.vector.tensor_tensor(wg[1][:], wg_raw[:], wg[0][:].bitcast(F32), ALU.subtract).then_inc(wg_lo, 1)
            nt.split_lo(dve)
            chain = Chain(dve, step_d, 0)
            dve.wait_ge(g_in, 48)
            dve.wait_ge(gate_done, 1)
            chain.link(nc.vector.tensor_tensor(logits[:], GT[:, 0:NT * E].rearrange("p (t e) -> p t e", e=E),
                                               bg[:].unsqueeze(1).broadcast_to([P, NT, E]), ALU.add))
            mine = logits[:].unsqueeze(3).broadcast_to([P, NT, E, E])
            other = logits[:].unsqueeze(2).broadcast_to([P, NT, E, E])
            nc.vector.tensor_tensor(beats[:], other, mine, ALU.is_gt)
            chain.link(nc.vector.tensor_tensor(ties[:], other, mine, ALU.is_equal))
            chain.link(nc.vector.tensor_tensor(ties[:], ties[:], pred[:].unsqueeze(1).broadcast_to([P, NT, E, E]),
                                               ALU.mult))
            chain.link(nc.vector.tensor_tensor(beats[:], beats[:], ties[:], ALU.add))
            chain.link(nc.vector.tensor_reduce(rank[:], beats[:], AX.X, ALU.add))
            nc.vector.tensor_scalar(share[:].rearrange("p (e t) -> p t e", t=NT), rank[:], 1.5, 0.5,
                                    ALU.is_lt, ALU.mult).then_inc(chosen, 1)
            dve.wait_ge(chosen, 1)
            dve.wait_ge(be_in, 16)

            def add(e, t):
                dve.wait_ge(relu_done, NT * e + t + 1)
                row = nt.row(t)
                nc.vector.tensor_tensor(row, act_out[:, t % 4, :], row, ALU.add).then_inc(added, 1)

            def expert(e, par, first=False):
                wait(dve, relu_done, NT * (e - 1))
                nc.vector.tensor_copy(cur[:, par, :], share[:, bass.ds(e * NT, NT)]).then_inc(picked, 1)
                for t in range(NT):
                    dve.wait_ge(item_done, NT * e + t + 1)
                    wait(dve, relu_done, NT * e + t - 3)
                    nc.vector.tensor_tensor(pre[:, t % 4, :], F[t % 4][:, :], be[:, bass.ds(e * D, D)],
                                            ALU.add).then_inc(biased, 1)
                    if t >= 2:
                        add(e, t - 2)
                    elif not first:
                        add(e - 1, t + NT - 2)

            expert(0, 0, first=True)
            expert(1, 1)
            with dve.Fori(1, E // 2) as n:
                expert(2 * n, 0)
                expert(2 * n + 1, 1)
            add(E - 1, NT - 2)
            add(E - 1, NT - 1)

            dve.wait_ge(added, NT * E)
            for t in range(NT):
                last = nc.vector.bn_stats(st6[:, t, :], nt.row(t))
            chain.link(last)
            for t in range(NT):
                last = nc.vector.bn_aggr(mv[:, t, :], st6[:, t, :])
            chain.link(last)
            rsqrt(nc, chain, mv[:, :, 1], rstd[:], tmp[:])
            for t in range(NT):
                nc.vector.tensor_scalar(nt.row(t), nt.row(t), mv[:, t, 0:1], rstd[:, t:t + 1],
                                        ALU.subtract, ALU.mult).then_inc(row_done, 1)

        @block.gpsimd
        def _(pool):
            def weights_lo(e, par):
                for c in range(C):
                    pool.wait_ge(we_hi, C * e + c + 1)
                    nc.gpsimd.tensor_tensor(we[1][:, par, c, :], raw[:, par, c, :], we[0][:, par, c, :].bitcast(F32),
                                            ALU.subtract).then_inc(we_lo, 1)

            weights_lo(0, 0)
            weights_lo(1, 1)
            with pool.Fori(1, E // 2) as n:
                weights_lo(2 * n, 0)
                weights_lo(2 * n + 1, 1)


def program(nc, io, out):
    with ExitStack() as ctx:
        top = {
            "x_tok": ctx.enter_context(nc.sbuf_tensor("x_tok", [P, NT * D], F32)),
            "ident": ctx.enter_context(nc.sbuf_tensor("ident", [P, P], F32)),
        }
        self_attention(nc, top, io["x_rows"], io["x_cols"], io["w_qkv"], io["w_out"], io["ln_cols"],
                       io["alibi"], io["head_rows"])
        xt = [ctx.enter_context(nc.sbuf_tensor(f"x_cols_{part}", [P, C, TOK], F32R)) for part in ("hi", "lo")]
        cross_attention(nc, top, xt, io["ctx_cols"], io["w_q"], io["w_kv"], io["w_d"], io["causal"])
        experts(nc, top, xt, io["w_gate"], io["b_gate"], io["w_e"], io["b_e"], io["before"], out)


def kernel(x, ctx_4096, L0_attn_Wqkv, L0_attn_q_ln_w, L0_attn_q_ln_b, L0_attn_k_ln_w, L0_attn_k_ln_b,
           L0_attn_Wout, L0_xattn_Wq, L0_xattn_Wk, L0_xattn_Wv, L0_xattn_Wd, L0_ffn_W_gate, L0_ffn_b_gate,
           L0_ffn_W_e, L0_ffn_b_e):
    import numpy as np
    import concourse.bacc as bacc
    from concourse.bass_utils import run_bass_kernel_spmd

    a = np.asarray
    rows = a(x).reshape(NT, P, D)
    slopes = 1.0 / np.power(2.0, np.arange(1, NH + 1, dtype=np.float32) * (8.0 / NH))
    rel = (np.arange(S)[None, :] - (np.arange(P) % S)[:, None]).astype(np.float32)
    hidden = np.where(rel <= 0, np.float32(0), np.float32(-1e30))
    alibi = np.where(rel[:, None, :] <= 0, slopes[None, :, None] * rel[:, None, :], np.float32(-1e30))
    lay = {
        "x_rows": rows.transpose(1, 0, 2),
        "x_cols": rows.reshape(NT, P, C, P).transpose(0, 3, 2, 1),
        "w_qkv": a(L0_attn_Wqkv).reshape(3, D, C, P).transpose(0, 2, 3, 1).reshape(3 * C, P, D),
        "w_out": a(L0_attn_Wout).reshape(D, C, P).transpose(1, 2, 0),
        "ln_cols": np.stack([a(v).reshape(C, P).T for v in
                             (L0_attn_q_ln_w, L0_attn_q_ln_b, L0_attn_k_ln_w, L0_attn_k_ln_b)], axis=1),
        "alibi": alibi.astype(np.float32),
        "causal": hidden.astype(np.float32),
        "head_rows": (np.arange(P)[:, None] // HD == np.arange(HPC)[None, :]).astype(np.float32),
        "before": np.broadcast_to((np.arange(E)[None, :] < np.arange(E)[:, None]).astype(np.float32), (P, E, E)),
        "ctx_cols": a(ctx_4096).reshape(2, HALF, C, P).transpose(2, 0, 3, 1),
        "w_q": a(L0_xattn_Wq).reshape(G, HG, DK, C, P).transpose(0, 1, 4, 3, 2).reshape(G, HG, P, C * DK),
        "w_kv": np.stack([a(w).reshape(G, DK, C, P).transpose(0, 3, 2, 1).reshape(G, P, C * DK)
                          for w in (L0_xattn_Wk, L0_xattn_Wv)], axis=1),
        "w_d": a(L0_xattn_Wd).reshape(D, G, HG, DK).transpose(1, 2, 3, 0),
        "w_gate": a(L0_ffn_W_gate).reshape(C, P, E).transpose(1, 0, 2),
        "b_gate": a(L0_ffn_b_gate).reshape(1, E),
        "w_e": a(L0_ffn_W_e).reshape(E, C, P, D),
        "b_e": a(L0_ffn_b_e).reshape(1, E * D),
    }
    nc = bacc.Bacc("TRN2", target_bir_lowering=False, num_devices=1)
    arrays, io = {}, {}
    for name, v in lay.items():
        arrays["in_" + name] = np.ascontiguousarray(v)
        io[name] = nc.dram_tensor("in_" + name, v.shape, F32, kind="ExternalInput").ap()
    out = nc.dram_tensor("out", (TOK, D), F32, kind="ExternalOutput").ap()
    program(nc, io, out.rearrange("(t p) d -> t p d", p=P))
    r = run_bass_kernel_spmd(nc, [arrays], core_ids=[0])
    return r.results[0]["out"].reshape(B, S, D)
```

```python
from contextlib import ExitStack

import concourse.bass as bass
from concourse import mybir

F32 = mybir.dt.float32
F32R = mybir.dt.float32r
I32 = mybir.dt.int32
ALU = mybir.AluOpType
ACT = mybir.ActivationFunctionType
AX = mybir.AxisListType

P = 128
B, S, D = 16, 64, 512
TOK = B * S
NT = TOK // P
C = D // P
NH, HD = 32, 16
HPC = P // HD
G, HG, DK = 8, 4, 128
HALF = TOK // 2
TH = NT // 2
E = 8
CLIP = 8.0
EPS = 1e-5
SLOTS = 8
RING = 5
RSQRT_MAGIC = 1597463007.0


class Chain:

    def __init__(self, eng, sem, base):
        self.eng, self.sem, self.base, self.k = eng, sem, base, 0

    def link(self, ins):
        self.k += 1
        ins.then_inc(self.sem, 1)
        self.eng.wait_ge(self.sem, self.base + self.k)


def wait(eng, sem, value):
    if not isinstance(value, int) or value > 0:
        eng.wait_ge(sem, value)


def products(nc, out, lhs, rhs, start=True, stop=True):
    (lh, ll), (rh, rl) = lhs, rhs
    nc.tensor.matmul(out, ll, rh, start=start, stop=False)
    nc.tensor.matmul(out, lh, rl, start=False, stop=False)
    return nc.tensor.matmul(out, lh, rh, start=False, stop=stop)


def rsqrt_start(nc, chain, var, y):
    chain.link(nc.vector.tensor_scalar(var, var, EPS, None, ALU.add))
    return nc.vector.tensor_scalar(y.bitcast(I32), var.bitcast(I32), -0.5, RSQRT_MAGIC, ALU.mult, ALU.add)


def rsqrt(nc, chain, var, y, t):
    chain.link(rsqrt_start(nc, chain, var, y))
    for _ in range(3):
        chain.link(nc.vector.tensor_tensor(t, y, y, ALU.mult))
        chain.link(nc.vector.scalar_tensor_tensor(t, t, -0.5, var, ALU.mult, ALU.mult))
        chain.link(nc.vector.scalar_tensor_tensor(y, t, 1.5, y, ALU.add, ALU.mult))


def self_attention(nc, top, nt, x_rows, x_cols, w_qkv, w_out, ln_cols, alibi_bias, head_rows, ctx_cols, w_q, w_kv):
    with ExitStack() as ctx:
        def sb(name, shape, dt=F32):
            return ctx.enter_context(nc.sbuf_tensor(name, shape, dt))

        def split(name, shape):
            return sb(name + "_hi", shape, F32R), sb(name + "_lo", shape, F32R)

        def sem(name):
            return ctx.enter_context(nc.semaphore(name))

        x_tok, ident = top["x_tok"], top["ident"]
        raw, wqkv = top["raw"], top["big"]
        wout = split("wout", [P, C, D])
        xt_raw = top["v_cols"][:].rearrange("p (c t) -> p c t", c=C)
        xt = split("xt", [P, C, P])
        qk_tok = sb("qk_tok", [P, 2, D])
        qk_col = sb("qk_col", [P, 2, C, P])
        k_col = [a[:].rearrange("p (c t) -> p c t", c=C) for a in top["k"]]
        v_tok = sb("v_tok", [P, 2, D])
        qz = split("qz", [P, C, 2, P])
        kblk = [a[:].rearrange("p c (b h t) -> p c b h t", b=2, h=HPC) for a in top["xt"]]
        v_pair = sb("v_pair", [P, NH // 2, 2, 2, 2, HD], F32R)
        probs = sb("probs", [P, NH, S])
        pt = split("pt", [P, 2, HPC // 2, P])
        att = sb("att", [P, D])
        ot = split("ot", [P, C, P])
        bias = sb("alibi", [P, NH, S])
        heads = sb("heads", [P, HPC])
        lnp = sb("lnp", [P, 4, C])
        st6 = sb("st6", [P, 2, 6])
        mv = sb("mv", [P, 2, 2])
        rstd = sb("rstd", [P, 2])
        tmp2 = sb("tmp2", [P, 2])
        halves = sb("halves", [P, 2, 2])
        mx = sb("mx", [P, NH])
        den = sb("den", [P, NH])

        def ps(name):
            return ctx.enter_context(nc.psum_tensor(name, [P, D], F32))

        R = [ps("aR0"), ps("aR1")]
        SC = [ps("aS0"), ps("aS1")]
        T = [ps("aT0"), ps("aT1")]
        O, Y = ps("aO"), ps("aY")
        OY = [O, Y]

        raw_in = [sem(f"raw_in{i}") for i in range(SLOTS)]
        w_hi = sem("w_hi")
        w_lo = [sem("w_lo_dve"), sem("w_lo_pool")]
        x_in, par_in, bias_in = sem("x_in"), sem("par_in"), sem("bias_in")
        xt_in, xt_hi, xt_lo = sem("xt_in"), sem("xt_hi"), sem("xt_lo")
        zeroed, ident_z, ident_in = sem("zeroed"), sem("ident_z"), sem("ident_in")
        qkv_done = sem("qkv_done")
        clipped = sem("clipped")
        v_swapped = sem("v_swapped")
        qk_normed = sem("qk_normed")
        qt_done, kt_done = sem("qt_done"), sem("kt_done")
        q_affine, k_affine = sem("q_affine"), sem("k_affine")
        qz_hi, qz_lo = sem("qz_hi"), sem("qz_lo")
        k_hi, k_split = sem("a_k_hi"), sem("k_split")
        kblk_hi, kblk_lo = sem("kblk_hi"), sem("kblk_lo")
        v_hi, v_lo = sem("a_v_hi"), sem("a_v_lo")
        scores_done = sem("scores_done")
        masked = sem("masked")
        row_max = sem("row_max")
        shifted = sem("shifted")
        exp_done = sem("exp_done")
        summed, inverse = sem("summed"), sem("inverse")
        pt_done = sem("pt_done")
        pt_hi, pt_lo = sem("pt_hi"), sem("pt_lo")
        pv_done = sem("pv_done")
        att_out = sem("att_out")
        att_scaled, att_done = sem("att_scaled"), sem("att_done")
        ot_hi, ot_lo = sem("ot_hi"), sem("ot_lo")
        y_done, y_added = sem("y_done"), sem("y_added")
        later_hi, later_lo = sem("later_hi"), sem("later_lo")
        step_0, step_n = sem("a_step_0"), sem("a_step_n")
        guessed, newton, inverted = sem("guessed"), sem("newton"), sem("inverted")

        def v_heads(b, h):
            return v_tok[h * S:(h + 1) * S, int(h != b), :].rearrange("p (r g d) -> p r g d", g=2, d=HD)[:, :, h, :]

        def v_place(part, b, h):
            return v_pair[h * S:(h + 1) * S, :, part, b, h, :]

        block = ctx.enter_context(nc.Block())
        NU = 3 * C + C
        LATER = range(2 * C + 2 + HG)
        BANKS = R + SC
        EARLY = range(NT - 2)

        def later_unit(part, m):
            if C <= m < C + 2:
                return top["wkv"][part][:, m - C, :]
            at = 2 * m if m < C else 2 * (m - C - 2) + 1 if m < 2 * C + 2 else m - 2
            return wqkv[part][:, at, :]

        def weight(n):
            return (wqkv, n) if n < 3 * C else (wout, n - 3 * C)

        @block.sync
        def _(sp):
            sp.dma_start(xt_raw, x_cols[0]).then_inc(xt_in, 16)
            for n in range(NU):
                if n >= SLOTS:
                    sp.wait_ge(w_lo[n % 2], (n - SLOTS) // 2 + 1)
                src = w_qkv[n] if n < 3 * C else w_out[n - 3 * C]
                sp.dma_start(raw[:, n % SLOTS, :], src).then_inc(raw_in[n % SLOTS], 16)

            def load_x(n):
                sp.wait_ge(xt_hi, n)
                sp.wait_ge(xt_lo, n)
                sp.dma_start(xt_raw, x_cols[n]).then_inc(xt_in, 16)

            load_x(1)
            sp.dma_start(lnp[:], ln_cols).then_inc(par_in, 16)
            sp.dma_start(heads[:], head_rows).then_inc(par_in, 16)
            sp.dma_start(bias[:], alibi_bias).then_inc(bias_in, 16)

            def swap_v(n):
                sp.wait_ge(clipped, 3 * n + 3)
                for h in range(2):
                    sp.dma_start(v_tok[h * S:(h + 1) * S, 1, :],
                                 v_tok[(1 - h) * S:(2 - h) * S, 0, :]).then_inc(v_swapped, 16)

            def load_later(m):
                src = (ctx_cols[m, 0] if m < C else w_kv[0, m - C] if m < C + 2 else
                       ctx_cols[m - C - 2, 1] if m < 2 * C + 2 else w_q[0, m - 2 * C - 2])
                sp.dma_start(raw[:, m % SLOTS, :], src).then_inc(raw_in[m % SLOTS], 16)

            swap_v(0)
            sp.dma_start(x_tok[:].rearrange("p (t d) -> p t d", t=NT), x_rows).then_inc(x_in, 16)
            for m in range(SLOTS):
                sp.wait_ge(w_lo[m % 2], (NU - SLOTS + m) // 2 + 1)
                load_later(m)
            with sp.Fori(2, NT) as n:
                load_x(n)
                swap_v(n - 1)
            swap_v(NT - 1)
            for m in LATER[SLOTS:]:
                sp.wait_ge(later_lo, m - SLOTS + 1)
                load_later(m)

        @block.tensor
        def _(pe):
            def project(n, js):
                pe.wait_ge(xt_hi, n + 1)
                pe.wait_ge(xt_lo, n + 1)
                for j in js:
                    wait(pe, clipped, 3 * n + max(j - 1, 0))
                    for c in range(C):
                        if isinstance(n, int) and n == 0:
                            unit = C * j + c
                            pe.wait_ge(w_lo[unit % 2], unit // 2 + 1)
                        last = products(nc, R[j % 2][:, :], [a[:, c, :] for a in xt],
                                        [a[:, C * j + c, :] for a in wqkv], start=(c == 0), stop=(c == C - 1))
                    last.then_inc(qkv_done, 1)

            def turn_k(n):
                pe.wait_ge(qk_normed, n + 1)
                wait(pe, k_affine, n)
                wait(pe, pt_lo, 4 * (n - 1))
                for c in range(C):
                    last = nc.tensor.transpose(T[1][:, c * P:(c + 1) * P], qk_tok[:, 1, c * P:(c + 1) * P], ident[:])
                last.then_inc(kt_done, 1)

            def turn_q(n):
                pe.wait_ge(qk_normed, n + 1)
                wait(pe, ot_lo, n - 1)
                for c in range(C):
                    last = nc.tensor.transpose(T[0][:, c * P:(c + 1) * P], qk_tok[:, 0, c * P:(c + 1) * P], ident[:])
                last.then_inc(qt_done, 1)

            def scores(i, cs):
                if 0 in cs:
                    pe.wait_ge(qz_hi, i + 1)
                    pe.wait_ge(qz_lo, i + 1)
                    pe.wait_ge(kblk_hi, i + 1)
                for c in cs:
                    pe.wait_ge(kblk_lo, 4 * i + c + 1)
                    wait(pe, masked, 4 * i + max(c - 1, 0))
                    for b in range(2):
                        last = products(nc, SC[c % 2][:, :], [a[:, c, b, :] for a in qz],
                                        [a[:, c, b, :, :] for a in kblk], start=(b == 0), stop=(b == 1))
                    last.then_inc(scores_done, 1)

            def turn_probs(i, c, more):
                pe.wait_ge(exp_done, 2 * i + c // 2 + 1)
                if c < 2:
                    wait(pe, (pt_lo, ot_lo)[c], (4 * i, i)[c])
                    if more:
                        pe.wait_ge((k_affine, q_affine)[c], i + 2)
                else:
                    pe.wait_ge(pt_lo, 4 * i + c - 1)
                for j in range(HPC // 2):
                    h = HPC * c + 2 * j
                    last = nc.tensor.transpose(T[1 - c % 2][:, j * P:(j + 1) * P], probs[:, h:h + 2, :], ident[:])
                last.then_inc(pt_done, 1)

            def weigh(i, c):
                pe.wait_ge(pt_hi, 4 * i + c + 1)
                pe.wait_ge(pt_lo, 4 * i + c + 1)
                if c == 0:
                    pe.wait_ge(v_hi, i + 1)
                    pe.wait_ge(v_lo, i + 1)
                if c == 1:
                    wait(pe, y_added, i)
                wait(pe, att_out, 4 * i + c - 1)
                for j in range(HPC // 2):
                    cols = OY[c % 2][:, j * P:(j + 1) * P]
                    v = v_pair[:, HPC // 2 * c + j, :, :, :, :]
                    nc.tensor.matmul(cols, pt[1][:, c % 2, j, :], v, start=True, stop=False)
                    last = nc.tensor.matmul(cols, pt[0][:, c % 2, j, :], v, start=False, stop=True)
                last.then_inc(pv_done, 1)

            def turn_att(i):
                pe.wait_ge(att_scaled, i + 1)
                pe.wait_ge(pt_lo, 4 * i + 4)
                for c in range(C):
                    last = nc.tensor.transpose(T[0][:, c * P:(c + 1) * P], att[:, c * P:(c + 1) * P], ident[:])
                last.then_inc(att_done, 1)

            def project_out(i):
                pe.wait_ge(ot_hi, i + 1)
                pe.wait_ge(ot_lo, i + 1)
                pe.wait_ge(att_out, 4 * i + 4)
                for c in range(C):
                    last = products(nc, Y[:, :], [a[:, c, :] for a in ot], [a[:, c, :] for a in wout],
                                    start=(c == 0), stop=(c == C - 1))
                last.then_inc(y_done, 1)

            def project_kv(j):
                pe.wait_ge(later_lo, C + j + 1)
                pe.wait_ge(nt.lo, 3 + j)
                for c in range(C):
                    last = products(nc, SC[j][:, :], [a[:, j, c * DK:(c + 1) * DK] for a in top["wkv"]],
                                    [a[:, 2 * c, :] for a in wqkv], start=(c == 0), stop=(c == C - 1))
                last.then_inc(top[("k_done", "v_done")[j]], 1)

            def step(i, before=True, one=True, two=True):
                scores(i, (0, 1))
                if one:
                    turn_k(i + 1)
                if before:
                    turn_att(i - 1)
                scores(i, (2, 3))
                if one:
                    turn_q(i + 1)
                if before:
                    project_out(i - 1)
                if two:
                    project(i + 2, (0,))
                if not one:
                    pe.wait_ge(clipped, 3 * NT)
                    nt.turn(pe, EARLY[0:2], BANKS)
                turn_probs(i, 0, one)
                if one:
                    turn_probs(i, 1, one)
                    if two:
                        project(i + 2, (1,))
                    weigh(i, 0)
                    turn_probs(i, 2, one)
                    weigh(i, 1)
                    turn_probs(i, 3, one)
                    if two:
                        project(i + 2, (2,))
                else:
                    weigh(i, 0)
                    turn_probs(i, 1, one)
                    turn_probs(i, 2, one)
                    pe.wait_ge(masked, 4 * NT)
                    nt.turn(pe, EARLY[2:4], BANKS)
                    weigh(i, 1)
                    turn_probs(i, 3, one)
                    nt.turn(pe, EARLY[4:6], BANKS)
                weigh(i, 2)
                weigh(i, 3)

            pe.wait_ge(ident_in, 1)
            project(0, range(3))
            turn_k(0)
            turn_q(0)
            project(1, range(3))
            for m in range(2):
                pe.wait_ge(w_lo[m], NU // 2)
            step(0, before=False)
            with pe.Fori(1, NT - 2) as i:
                step(i)
            step(NT - 2, two=False)
            step(NT - 1, one=False, two=False)
            project_kv(0)
            turn_att(NT - 1)
            project_kv(1)
            project_out(NT - 1)

        @block.scalar
        def _(act):
            def split_x(n):
                act.wait_ge(xt_in, 16 * n + 16)
                wait(act, qkv_done, 3 * n)
                nc.scalar.activation(xt[0][:], xt_raw, ACT.Copy).then_inc(xt_hi, 1)

            def affine(n, j):
                act.wait_ge((qt_done, kt_done)[j], n + 1)
                wait(act, (qz_lo, k_split)[j], n)
                for c in range(C):
                    last = nc.scalar.activation(qk_col[:, j, c, :], T[j][:, c * P:(c + 1) * P], ACT.Identity,
                                                bias=lnp[:, 2 * j + 1, c:c + 1], scale=lnp[:, 2 * j, c:c + 1])
                last.then_inc((q_affine, k_affine)[j], 1)

            def split_k(n):
                act.wait_ge(k_affine, n + 1)
                nc.scalar.activation(k_col[0], qk_col[:, 1, :, :], ACT.Copy).then_inc(k_hi, 1)

            def spread_q(n):
                wait(act, scores_done, 4 * n)
                act.wait_ge(q_affine, n + 1)
                for b in range(2):
                    last = nc.scalar.activation(qz[0][:, :, b, b * S:(b + 1) * S],
                                                qk_col[:, 0, :, b * S:(b + 1) * S], ACT.Copy)
                last.then_inc(qz_hi, 1)

            def spread_k(n, hs):
                if 0 in hs:
                    act.wait_ge(k_hi, n + 1)
                    wait(act, scores_done, 4 * n)
                for h in hs:
                    last = nc.scalar.activation(kblk[0][:, :, :, h, :],
                                                k_col[0].bitcast(F32).rearrange("p c (b t) -> p c b t", b=2),
                                                ACT.Copy, scale=heads[:, h:h + 1])
                if HPC - 1 in hs:
                    last.then_inc(kblk_hi, 1)

            def spread_v(n):
                act.wait_ge(v_swapped, 32 * n + 32)
                wait(act, pv_done, 4 * n)
                for b in range(2):
                    for h in range(2):
                        last = nc.scalar.activation(v_place(0, b, h), v_heads(b, h), ACT.Copy)
                last.then_inc(v_hi, 1)

            def exps(i, f):
                act.wait_ge(shifted, 2 * i + f + 1)
                v = probs[:, f * NH // 2:(f + 1) * NH // 2, :]
                nc.scalar.activation(v, v, ACT.Exp).then_inc(exp_done, 1)

            def probs_hi(i, c):
                act.wait_ge(pt_done, 4 * i + c + 1)
                wait(act, pv_done, 4 * i + max(c - 1, 0))
                nc.scalar.activation(pt[0][:, c % 2, :, :], T[1 - c % 2][:, :], ACT.Copy).then_inc(pt_hi, 1)

            def att_hi(i):
                act.wait_ge(att_done, i + 1)
                wait(act, y_done, i)
                nc.scalar.activation(ot[0][:], T[0][:, :], ACT.Copy).then_inc(ot_hi, 1)

            def later(ms):
                for m in ms:
                    act.wait_ge(raw_in[m % SLOTS], 16 * ((NU + m) // SLOTS) + 16)
                    if m == 0:
                        act.wait_ge(qkv_done, 3 * NT)
                    nc.scalar.activation(later_unit(0, m), raw[:, m % SLOTS, :], ACT.Copy).then_inc(later_hi, 1)

            def step(i, before=True, one=True, two=True):
                if two:
                    split_x(i + 2)
                if not one:
                    act.wait_ge(nt.shifted, 1)
                    nt.norm_act(EARLY[0:3], nt.normed)
                if before:
                    att_hi(i - 1)
                if not one:
                    nt.norm_act(EARLY[3:], nt.normed)
                if one:
                    affine(i + 1, 1)
                    split_k(i + 1)
                exps(i, 0)
                if one:
                    affine(i + 1, 0)
                if not one:
                    later(LATER[3:5])
                if not two:
                    probs_hi(i, 0)
                if one and not two:
                    probs_hi(i, 1)
                exps(i, 1)
                if one:
                    spread_q(i + 1)
                    spread_k(i + 1, (0, 1))
                    for c in range(C):
                        if two or c > 1:
                            probs_hi(i, c)
                        if c > 0:
                            spread_k(i + 1, (2 * c, 2 * c + 1))
                    spread_v(i + 1)
                    if not two:
                        later(LATER[0:3])
                else:
                    probs_hi(i, 1)
                    nt.split_hi(act, EARLY[0:4], BANKS)
                    probs_hi(i, 2)
                    later(LATER[5:7])
                    probs_hi(i, 3)
                    nt.split_hi(act, EARLY[4:6], BANKS)

            split_x(0)
            for n in range(NU):
                act.wait_ge(raw_in[n % SLOTS], 16 * (n // SLOTS) + 16)
                w, at = weight(n)
                nc.scalar.activation(w[0][:, at, :], raw[:, n % SLOTS, :], ACT.Copy).then_inc(w_hi, 1)
            split_x(1)
            act.wait_ge(par_in, 32)
            act.wait_ge(zeroed, 3)
            affine(0, 1)
            split_k(0)
            affine(0, 0)
            spread_q(0)
            spread_k(0, range(HPC))
            spread_v(0)
            step(0, before=False)
            with act.Fori(1, NT - 2) as i:
                step(i)
            step(NT - 2, two=False)
            step(NT - 1, one=False, two=False)
            later(LATER[7:])
            act.wait_ge(top["k_done"], 1)
            nc.scalar.activation(top["k"][0][:], SC[0][:, :], ACT.Copy).then_inc(top["k_hi"], 1)
            att_hi(NT - 1)
            act.wait_ge(top["v_done"], 1)
            nc.scalar.activation(top["v_cols"][:], SC[1][:, :], ACT.Copy).then_inc(top["vt_out"], 1)

        @block.vector
        def _(dve):
            STEPS_N = 3

            def clip(n, item, dst):
                dve.wait_ge(qkv_done, 3 * n + item + 1)
                nc.vector.tensor_scalar(dst, R[item % 2][:, :], CLIP, -CLIP, ALU.min, ALU.max).then_inc(clipped, 1)

            def clip_v(n):
                wait(dve, v_hi, n)
                wait(dve, v_lo, n)
                clip(n, 2, v_tok[:, 0, :])

            def clip_q(n):
                wait(dve, qt_done, n)
                clip(n, 0, qk_tok[:, 0, :])

            def stats(n, chain):
                wait(dve, kt_done, n)
                clip(n, 1, qk_tok[:, 1, :])
                dve.wait_ge(clipped, 3 * n + 2)
                for j in range(2):
                    last = nc.vector.bn_stats(st6[:, j, :], qk_tok[:, j, :])
                chain.link(last)
                nc.vector.memset(tmp2[:], 0.0)
                for j in range(2):
                    last = nc.vector.bn_aggr(mv[:, j, :], st6[:, j, :])
                chain.link(last)

            def norm(n):
                wait(dve, inverted, n - 1)
                for j in range(2):
                    last = nc.vector.tensor_scalar(qk_tok[:, j, :], qk_tok[:, j, :], mv[:, j, 0:1], rstd[:, j:j + 1],
                                                   ALU.subtract, ALU.mult)
                last.then_inc(qk_normed, 1)

            def k_lo(n):
                dve.wait_ge(k_hi, n + 1)
                wait(dve, kblk_lo, 4 * n)
                nc.vector.tensor_tensor(k_col[1], qk_col[:, 1, :, :], k_col[0].bitcast(F32),
                                        ALU.subtract).then_inc(k_split, 1)

            def spread_v(n):
                dve.wait_ge(v_hi, n + 1)
                for b in range(2):
                    for h in range(2):
                        last = nc.vector.tensor_tensor(v_place(1, b, h), v_heads(b, h),
                                                       v_place(0, b, h).bitcast(F32), ALU.subtract)
                last.then_inc(v_lo, 1)

            def half(f):
                return slice(f * NH // 2, (f + 1) * NH // 2)

            def mask(i, cs):
                if 0 in cs:
                    wait(dve, pt_done, 4 * i)
                for c in cs:
                    dve.wait_ge(scores_done, 4 * i + c + 1)
                    hs = slice(HPC * c, HPC * (c + 1))
                    nc.vector.scalar_tensor_tensor(probs[:, hs, :], SC[c % 2][:, :].rearrange("p (h k) -> p h k", k=S),
                                                   HD ** -0.5, bias[:, hs, :], ALU.mult, ALU.add).then_inc(masked, 1)

            def row_max_of(i, f):
                dve.wait_ge(masked, 4 * i + 2 * f + 2)
                nc.vector.tensor_reduce(mx[:, half(f)], probs[:, half(f), :], AX.X, ALU.max).then_inc(row_max, 1)

            def sums(i, f):
                if f == 0:
                    wait(dve, att_scaled, i)
                dve.wait_ge(exp_done, 2 * i + f + 1)
                nc.vector.tensor_reduce(den[:, half(f)], probs[:, half(f), :], AX.X, ALU.add).then_inc(summed, 1)

            def invert(i):
                dve.wait_ge(summed, 2 * i + 2)
                nc.vector.reciprocal(den[:], den[:]).then_inc(inverse, 1)

            def probs_lo(i, c):
                dve.wait_ge(pt_hi, 4 * i + c + 1)
                nc.vector.tensor_tensor(pt[1][:, c % 2, :, :].rearrange("p j t -> p (j t)"), T[1 - c % 2][:, :],
                                        pt[0][:, c % 2, :, :].rearrange("p j t -> p (j t)").bitcast(F32),
                                        ALU.subtract).then_inc(pt_lo, 1)

            def gather(i, c):
                dve.wait_ge(pv_done, 4 * i + c + 1)
                if c == 0:
                    wait(dve, att_done, i)
                for b in range(2):
                    rows = slice(b * S, (b + 1) * S)
                    parts = OY[c % 2][rows, :].rearrange("p (j x b gd) -> p j b gd x", x=2, b=2, gd=2 * HD)[:, :, b, :, :]
                    last = nc.vector.tensor_reduce(att[rows, c * P:(c + 1) * P].rearrange("p (j gd) -> p j gd", gd=2 * HD),
                                                   parts, AX.X, ALU.add)
                last.then_inc(att_out, 1)

            def att_lo(i):
                dve.wait_ge(ot_hi, i + 1)
                nc.vector.tensor_tensor(ot[1][:].rearrange("p c t -> p (c t)"), T[0][:, :],
                                        ot[0][:].rearrange("p c t -> p (c t)").bitcast(F32),
                                        ALU.subtract).then_inc(ot_lo, 1)

            def add_out(i):
                dve.wait_ge(y_done, i + 1)
                rows = x_tok[:, bass.ds(i * D, D)]
                nc.vector.tensor_tensor(rows, Y[:, :], rows, ALU.add).then_inc(y_added, 1)

            def step(i, before=True, one=True, two=True):
                mask(i, (0, 1))
                row_max_of(i, 0)
                if before:
                    att_lo(i - 1)
                spread_v(i)
                mask(i, (2, 3))
                row_max_of(i, 1)
                if one:
                    clip_v(i + 1)
                    k_lo(i + 1)
                sums(i, 0)
                if not two:
                    probs_lo(i, 0)
                if one and not two:
                    probs_lo(i, 1)
                if before:
                    add_out(i - 1)
                if two:
                    clip_q(i + 2)
                    probs_lo(i, 0)
                if two or not one:
                    probs_lo(i, 1)
                sums(i, 1)
                invert(i)
                if two:
                    chain = Chain(dve, step_n, STEPS_N * i)
                    stats(i + 2, chain)
                    rsqrt_start(nc, chain, mv[:, :, 1], rstd[:]).then_inc(guessed, 1)
                gather(i, 0)
                probs_lo(i, 2)
                if not two:
                    nt.stats(dve, EARLY[0:3]) if one else nt.split_lo(dve, EARLY[0:2], BANKS)
                gather(i, 1)
                probs_lo(i, 3)
                if two:
                    norm(i + 2)
                elif one:
                    nt.stats(dve, EARLY[3:])
                    nt.invert(dve, EARLY)
                    nt.shift(EARLY)
                else:
                    nt.split_lo(dve, EARLY[2:4], BANKS)
                gather(i, 2)
                gather(i, 3)

            def weights_lo(ns):
                for n in ns:
                    dve.wait_ge(w_hi, n + 1)
                    w, at = weight(n)
                    nc.vector.tensor_tensor(w[1][:, at, :], raw[:, n % SLOTS, :], w[0][:, at, :].bitcast(F32),
                                            ALU.subtract).then_inc(w_lo[0], 1)

            weights_lo((0, 2, 4, 6))
            for a in (qz[0], qz[1], v_pair):
                nc.vector.memset(a[:].bitcast(F32), 0.0).then_inc(zeroed, 1)
            weights_lo(range(8, 3 * C, 2))
            chain0 = Chain(dve, step_0, 0)
            clip_q(0)
            stats(0, chain0)
            rsqrt(nc, chain0, mv[:, :, 1], rstd[:], tmp2[:])
            norm(0)
            clip_v(0)
            weights_lo(range(3 * C, NU, 2))
            k_lo(0)
            clip_q(1)
            stats(1, chain0)
            rsqrt(nc, chain0, mv[:, :, 1], rstd[:], tmp2[:])
            norm(1)
            dve.wait_ge(bias_in, 16)
            step(0, before=False)
            dve.wait_ge(x_in, 16)
            with dve.Fori(1, NT - 2) as i:
                step(i)
            step(NT - 2, two=False)
            step(NT - 1, one=False, two=False)
            nt.split_lo(dve, EARLY[4:6], BANKS)
            nt.stats(dve, [NT - 2])
            dve.wait_ge(top["k_hi"], 1)
            nc.vector.tensor_tensor(top["k"][1][:], SC[0][:, :], top["k"][0][:].bitcast(F32),
                                    ALU.subtract).then_inc(top["k_lo"], 1)
            att_lo(NT - 1)
            add_out(NT - 1)

        @block.gpsimd
        def _(pool):
            def split_x(n):
                pool.wait_ge(xt_hi, n + 1)
                nc.gpsimd.tensor_tensor(xt[1][:], xt_raw, xt[0][:].bitcast(F32), ALU.subtract).then_inc(xt_lo, 1)

            def spread_k(n):
                pool.wait_ge(k_split, n + 1)
                wait(pool, scores_done, 4 * n)
                for c in range(C):
                    k = k_col[1][:, c, :].bitcast(F32).rearrange("p (b t) -> p b t", b=2).unsqueeze(2)
                    nc.gpsimd.tensor_tensor(kblk[1][:, c, :, :, :], k.broadcast_to([P, 2, HPC, S]),
                                            heads[:].unsqueeze(1).unsqueeze(3).broadcast_to([P, 2, HPC, S]),
                                            ALU.mult).then_inc(kblk_lo, 1)

            def spread_q(n):
                pool.wait_ge(qz_hi, n + 1)
                for b in range(2):
                    cols = slice(b * S, (b + 1) * S)
                    last = nc.gpsimd.tensor_tensor(qz[1][:, :, b, cols], qk_col[:, 0, :, cols],
                                                   qz[0][:, :, b, cols].bitcast(F32), ALU.subtract)
                last.then_inc(qz_lo, 1)

            def invert(n):
                pool.wait_ge(guessed, n - 1)
                var, y, t = mv[:, :, 1], rstd[:], tmp2[:]
                chain = Chain(pool, newton, 12 * (n - 2))
                chain.link(nc.gpsimd.tensor_tensor(var, var, halves[:, 0, :], ALU.mult))
                for k in range(3):
                    chain.link(nc.gpsimd.tensor_tensor(t, y, y, ALU.mult))
                    chain.link(nc.gpsimd.tensor_tensor(t, t, var, ALU.mult))
                    chain.link(nc.gpsimd.tensor_tensor(t, t, halves[:, 1, :], ALU.add))
                    last = nc.gpsimd.tensor_tensor(y, t, y, ALU.mult)
                    if k < 2:
                        chain.link(last)
                last.then_inc(inverted, 1)

            def shift(i, f):
                hf = slice(f * NH // 2, (f + 1) * NH // 2)
                v = probs[:, hf, :]
                pool.wait_ge(row_max, 2 * i + f + 1)
                nc.gpsimd.tensor_tensor(v, v, mx[:, hf].unsqueeze(2).broadcast_to([P, NH // 2, S]),
                                        ALU.subtract).then_inc(shifted, 1)

            def scale(i):
                pool.wait_ge(inverse, i + 1)
                pool.wait_ge(att_out, 4 * i + 4)
                v = att[:].rearrange("p (h d) -> p h d", d=HD)
                nc.gpsimd.tensor_tensor(v, v, den[:].unsqueeze(2).broadcast_to([P, NH, HD]),
                                        ALU.mult).then_inc(att_scaled, 1)

            def later(ms):
                for m in ms:
                    pool.wait_ge(later_hi, m + 1)
                    nc.gpsimd.tensor_tensor(later_unit(1, m), raw[:, m % SLOTS, :],
                                            later_unit(0, m).bitcast(F32), ALU.subtract).then_inc(later_lo, 1)

            def step(i, one=True, two=True):
                if two:
                    split_x(i + 2)
                shift(i, 0)
                shift(i, 1)
                if one:
                    spread_k(i + 1)
                    spread_q(i + 1)
                if two:
                    invert(i + 2)
                if not one:
                    later(LATER[3:9])
                scale(i)
                if not two:
                    later(LATER[0:3] if one else LATER[9:])

            nc.gpsimd.memset(halves[:, 0, :], -0.5)
            nc.gpsimd.memset(halves[:, 1, :], 1.5)
            nc.gpsimd.memset(ident[:], 0.0).then_inc(ident_z, 1)
            pool.wait_ge(ident_z, 1)
            nc.gpsimd.affine_select(out=ident[:], in_=ident[:], compare_op=ALU.not_equal, fill=1.0, base=0,
                                    pattern=[[-1, P]], channel_multiplier=1).then_inc(ident_in, 1)
            split_x(0)
            for n in range(1, NU, 2):
                pool.wait_ge(w_hi, n + 1)
                w, at = weight(n)
                nc.gpsimd.tensor_tensor(w[1][:, at, :], raw[:, n % SLOTS, :], w[0][:, at, :].bitcast(F32),
                                        ALU.subtract).then_inc(w_lo[1], 1)
            split_x(1)
            pool.wait_ge(zeroed, 3)
            pool.wait_ge(par_in, 32)
            spread_q(0)
            spread_k(0)
            step(0)
            with pool.Fori(1, NT - 2) as i:
                step(i)
            step(NT - 2, two=False)
            step(NT - 1, one=False, two=False)


class NormTurn:

    def __init__(self, nc, ctx, name, top):
        self.nc, self.x_tok, self.ident, self.xt = nc, top["x_tok"], top["ident"], top["xt"]

        def sb(part, shape):
            return ctx.enter_context(nc.sbuf_tensor(name + part, shape, F32))

        self.st6, self.mv = sb("_st6", [P, NT, 6]), sb("_mv", [P, NT, 2])
        self.rstd, self.tmp = sb("_rstd", [P, NT]), sb("_tmp", [P, NT])
        self.step, self.normed, self.turned, self.hi, self.lo, self.shifted, self.normed_act = [
            ctx.enter_context(nc.semaphore(name + part))
            for part in ("_step", "_normed", "_turned", "_hi", "_lo", "_shifted", "_normed_act")]
        self.steps = 0

    def row(self, t):
        return self.x_tok[:, t * D:(t + 1) * D]

    def stats(self, dve, ts):
        nc, chain = self.nc, Chain(dve, self.step, self.steps)
        for t in ts:
            last = nc.vector.bn_stats(self.st6[:, t, :], self.row(t))
        chain.link(last)
        for t in ts:
            last = nc.vector.bn_aggr(self.mv[:, t, :], self.st6[:, t, :])
        chain.link(last)
        self.steps += chain.k

    def invert(self, dve, ts):
        chain, cols = Chain(dve, self.step, self.steps), slice(ts[0], ts[-1] + 1)
        rsqrt(self.nc, chain, self.mv[:, cols, 1], self.rstd[:, cols], self.tmp[:, cols])
        self.steps += chain.k

    def shift(self, ts):
        cols = slice(ts[0], ts[-1] + 1)
        self.nc.vector.scalar_tensor_tensor(self.tmp[:, cols], self.mv[:, cols, 0], -1.0, self.rstd[:, cols],
                                            ALU.mult, ALU.mult).then_inc(self.shifted, 1)

    def norm_act(self, ts, done):
        for t in ts:
            self.nc.scalar.activation(self.row(t), self.row(t), ACT.Identity, bias=self.tmp[:, t:t + 1],
                                      scale=self.rstd[:, t:t + 1]).then_inc(done, 1)

    def norm(self, ts):
        for t in ts:
            self.nc.vector.tensor_scalar(self.row(t), self.row(t), self.mv[:, t, 0:1], self.rstd[:, t:t + 1],
                                         ALU.subtract, ALU.mult).then_inc(self.normed, 1)

    def turn(self, pe, ts, banks):
        for t in ts:
            pe.wait_ge(self.normed, t + 1)
            wait(pe, self.lo, t - len(banks) + 1)
            for c in range(C):
                last = self.nc.tensor.transpose(banks[t % len(banks)][:, c * P:(c + 1) * P],
                                                self.row(t)[:, c * P:(c + 1) * P], self.ident[:])
            last.then_inc(self.turned, 1)

    def split_hi(self, act, ts, banks):
        for t in ts:
            act.wait_ge(self.turned, t + 1)
            self.nc.scalar.activation(self.xt[0][:, :, t * P:(t + 1) * P],
                                      banks[t % len(banks)][:, :].rearrange("p (c t) -> p c t", c=C),
                                      ACT.Copy).then_inc(self.hi, 1)

    def split_lo(self, dve, ts, banks):
        for t in ts:
            dve.wait_ge(self.hi, t + 1)
            self.nc.vector.tensor_tensor(self.xt[1][:, :, t * P:(t + 1) * P],
                                         banks[t % len(banks)][:, :].rearrange("p (c t) -> p c t", c=C),
                                         self.xt[0][:, :, t * P:(t + 1) * P].bitcast(F32),
                                         ALU.subtract).then_inc(self.lo, 1)


def cross_attention(nc, top, nt, nt2, w_q, w_kv, w_d, causal_bias, w_e):
    with ExitStack() as ctx:
        def sb(name, shape, dt=F32):
            return ctx.enter_context(nc.sbuf_tensor(name, shape, dt))

        def split(name, shape):
            return sb(name + "_hi", shape, F32R), sb(name + "_lo", shape, F32R)

        def sem(name):
            return ctx.enter_context(nc.semaphore(name))

        x_tok, ident = top["x_tok"], top["ident"]
        raw, xt = top["raw"], top["xt"]
        ct = [a[:, 0:2 * C, :].rearrange("p (c x) d -> p c (x d)", x=2) for a in top["big"]]
        wq = [a[:, 2 * C:2 * C + HG, :].rearrange("p h (c d) -> p h c d", c=C) for a in top["big"]]
        wkv = [a[:].rearrange("p j (c d) -> p j c d", c=C) for a in top["wkv"]]
        wd = split("wd", [P, HG, D])
        q = split("q", [P, 2 * TH, HG, S])
        k, v_cols = top["k"], top["v_cols"]
        v = split("v", [P, 2, TH, DK])
        st = sb("scores_t", [P, TH, HG * S])
        probs = sb("c_probs", [P, TH, 2, 2, S])
        pt = split("c_pt", [P, 2, 2, HG * S])
        ot = split("c_ot", [P, HG, HALF])
        mask = sb("causal", [P, S])
        mx = sb("c_mx", [P, 4 * TH])
        den = sb("c_den", [P, 4 * TH])

        def ps(name):
            return ctx.enter_context(nc.psum_tensor(name, [P, D], F32))

        R = [ps("cR0"), ps("cR1")]
        SC = [ps("cS0"), ps("cS1")]
        T = [ps("cT0"), ps("cT1")]
        O = [ps("cO0"), ps("cO1")]
        BANKS, LATE = SC + T, range(NT - 2, NT)

        raw_in = [sem(f"c_raw_in{i}") for i in range(RING)]
        mask_in = sem("mask_in")
        w_hi, w_lo = sem("c_w_hi"), sem("c_w_lo")
        k_done, v_done, k_hi, k_lo, vt_out = [top[name] for name in ("k_done", "v_done", "k_hi", "k_lo", "vt_out")]
        q_done, y_done, vt_done = sem("q_done"), sem("c_y_done"), sem("vt_done")
        q_hi, v_hi = sem("q_hi"), sem("v_hi")
        q_lo, v_lo, y_added = sem("q_lo"), sem("v_lo"), sem("c_y_added")
        keyed, st_out = sem("c_keyed"), sem("c_st_out")
        scores_done, masked, row_max = sem("c_scores_done"), sem("c_masked"), sem("c_row_max")
        shifted, exp_done, summed = sem("c_shifted"), sem("c_exp_done"), sem("c_summed")
        inverse, probs_done = sem("c_inverse"), sem("c_probs_done")
        pt_done, pt_hi, pt_lo = sem("c_pt_done"), sem("c_pt_hi"), sem("c_pt_lo")
        pv_done, o_hi, o_lo = sem("c_pv_done"), sem("c_o_hi"), sem("c_o_lo")

        EARLY = range(TH)
        we = [a[:, 0:2 * C, :] for a in top["big"]]

        PER = 2 * HG + 2

        def unit(g, j):
            return PER * g + j

        def slot(j):
            return j % RING, j // RING

        def out_cols(a, u, b):
            return a[:].rearrange("p h (t b s) -> p t h b s", t=TH, b=2)[:, 2 * u:2 * u + 2, :, b, :]

        block = ctx.enter_context(nc.Block())

        @block.sync
        def _(sp):
            sp.dma_start(mask[:], causal_bias).then_inc(mask_in, 16)

            def stream(g):
                for j in range(PER):
                    if j >= HG and isinstance(g, int) and g == G - 1:
                        return
                    wait(sp, w_lo, unit(g, j) - RING + 1)
                    src = w_d[g, j] if j < HG else w_q[g + 1, j - HG] if j < 2 * HG else w_kv[g + 1, j - 2 * HG]
                    sp.dma_start(raw[:, slot(j)[0], :], src).then_inc(raw_in[slot(j)[0]], 16)

            stream(0)
            with sp.Fori(1, G - 1) as g:
                stream(g)
            stream(G - 1)
            sp.wait_ge(w_lo, unit(G - 1, HG))
            for e in range(2):
                sp.dma_start(raw[:, e * C:(e + 1) * C, :],
                             w_e[e].rearrange("c p h -> p c h")).then_inc(top["we_in"][e], 16)

        @block.tensor
        def _(pe):
            def project_q(p, g, hf):
                for h in range(HG):
                    wait(pe, w_lo, PER * (g - 1) + HG + h + 1)
                    if h < 2:
                        if isinstance(p, int) and p == 0:
                            wait(pe, v_lo, h)
                        elif isinstance(p, int) and p == 1:
                            pe.wait_ge((k_lo, v_lo)[h], 1)
                        else:
                            wait(pe, y_added, 4 * p - 5 + h)
                    else:
                        pe.wait_ge(q_lo, 4 * p + h - 1)
                    for c in range(C):
                        last = products(nc, R[h % 2][:, :], [a[:, h, c, :] for a in wq],
                                        [a[:, c, hf * HALF:(hf + 1) * HALF] for a in xt],
                                        start=(c == 0), stop=(c == C - 1))
                    last.then_inc(q_done, 1)

            def project_k(p, g, hf):
                wait(pe, w_lo, PER * (g - 1) + 2 * HG + 1)
                pe.wait_ge(q_lo, 4 * p + 3)
                for c in range(C):
                    last = products(nc, R[0][:, :], [a[:, 0, c, :] for a in wkv],
                                    [a[:, c, hf * HALF:(hf + 1) * HALF] for a in ct],
                                    start=(c == 0), stop=(c == C - 1))
                last.then_inc(k_done, 1)

            def project_v(p, g, hf):
                wait(pe, w_lo, PER * (g - 1) + 2 * HG + 2)
                pe.wait_ge(q_lo, 4 * p + 4)
                for c in range(C):
                    last = products(nc, R[1][:, :], [a[:, 1, c, :] for a in wkv],
                                    [a[:, c, hf * HALF:(hf + 1) * HALF] for a in ct],
                                    start=(c == 0), stop=(c == C - 1))
                last.then_inc(v_done, 1)

            def turn_v(p):
                pe.wait_ge(vt_out, p + 1)
                for t in range(TH):
                    last = nc.tensor.transpose(R[1][:, t * DK:(t + 1) * DK], v_cols[:, t * P:(t + 1) * P], ident[:])
                last.then_inc(vt_done, 1)

            def scores(s, ts):
                pe.wait_ge(q_lo, 4 * s + 4)
                pe.wait_ge(k_lo, s + 1)
                for t in ts:
                    wait(pe, st_out, 4 * s + t - 1)
                    last = products(nc, SC[t % 2][:, :], [a[:, t * P:(t + 1) * P] for a in k],
                                    [a[:, 2 * t:2 * t + 2, :, :] for a in q])
                    last.then_inc(keyed, 1)

            def turn_scores(s):
                wait(pe, pt_lo, 2 * s)
                for u in range(2):
                    pe.wait_ge(st_out, 4 * s + 2 * u + 2)
                    for t in (2 * u, 2 * u + 1):
                        for r in range(2):
                            col = (t % 2) * 256 + r * 128
                            last = nc.tensor.transpose(T[u][:, col:col + P], st[:, t, r * P:(r + 1) * P], ident[:])
                    last.then_inc(scores_done, 1)

            def turn(s):
                pe.wait_ge(probs_done, s + 1)
                for u in range(2):
                    for t in (2 * u, 2 * u + 1):
                        for r in range(2):
                            col = (t % 2) * 256 + r * 128
                            last = nc.tensor.transpose(T[u][:, col:col + P], probs[:, t, r, :, :], ident[:])
                    last.then_inc(pt_done, 1)

            def weigh(s, u, par):
                pe.wait_ge(pt_lo, 2 * s + u + 1)
                pe.wait_ge(v_lo, s + 1)
                for t in range(2):
                    for i, (lv, lp) in enumerate(((1, 0), (0, 1), (0, 0))):
                        for b in range(2):
                            rows = slice(b * S, (b + 1) * S)
                            if t == 0 and i == 0:
                                wait(pe, o_lo, 4 * s + 2 * u + b - 1)
                            last = nc.tensor.matmul(O[b][:, t * 256:(t + 1) * 256], v[lv][rows, par, 2 * u + t, :],
                                                    pt[lp][rows, u, t, :], start=(i == 0), stop=(i == 2))
                last.then_inc(pv_done, 1)

            def project_out(s, g, more):
                pe.wait_ge(w_lo, PER * g + HG)
                pe.wait_ge(o_lo, 4 * s + 4)
                for t in range(TH):
                    if t < 2 and more:
                        pe.wait_ge((k_lo, v_lo)[t], s + 2)
                    else:
                        pe.wait_ge(y_added, 4 * s + t - 1)
                    for h in range(HG):
                        last = products(nc, R[t % 2][:, :], [a[:, h, t * P:(t + 1) * P] for a in ot],
                                        [a[:, h, :] for a in wd], start=(h == 0), stop=(h == HG - 1))
                    last.then_inc(y_done, 1)
                    if t == 0 and more:
                        turn_scores(s + 1)
                    elif t == 0:
                        nt2.turn(pe, EARLY[2:], BANKS)

            def step(s, g, hf, more=True):
                g1, hf1 = (g, 1) if hf == 0 else (g + 1, 0)
                if more:
                    project_q(s + 1, g1, hf1)
                turn(s)
                if more:
                    project_k(s + 1, g1, hf1)
                weigh(s, 0, hf)
                if more:
                    project_v(s + 1, g1, hf1)
                weigh(s, 1, hf)
                if more:
                    scores(s + 1, (0, 1))
                    turn_v(s + 1)
                    scores(s + 1, (2, 3))
                else:
                    nt2.turn(pe, EARLY[0:2], BANKS)
                project_out(s, g, more)

            turn_v(0)
            project_q(0, 0, 0)
            nt.turn(pe, LATE, BANKS)
            scores(0, (0, 1))
            scores(0, (2, 3))
            pe.wait_ge(nt.lo, NT)
            turn_scores(0)
            step(0, 0, 0)
            step(1, 0, 1)
            with pe.Fori(1, G - 1) as g:
                step(2 * g, g, 0)
                step(2 * g + 1, g, 1)
            step(2 * G - 2, G - 1, 0)
            step(2 * G - 1, G - 1, 1, more=False)

        @block.scalar
        def _(act):
            def weights_hi(g, js):
                for j in js:
                    n, use = slot(j)
                    act.wait_ge(raw_in[n], 16 * (2 * g + use) + 16)
                    src = raw[:, n, :]
                    if j < HG:
                        wait(act, y_done, 8 * g)
                        dst = wd[0][:, j, :]
                    elif j < 2 * HG:
                        act.wait_ge(q_done, 8 * g + 8)
                        dst = wq[0][:, j - HG, :, :].rearrange("p c d -> p (c d)")
                    else:
                        act.wait_ge(k_done if j == 2 * HG else v_done, 2 * g + 2)
                        dst = wkv[0][:, j - 2 * HG, :, :].rearrange("p c d -> p (c d)")
                    nc.scalar.activation(dst, src, ACT.Copy).then_inc(w_hi, 1)

            def q_split(p, hs=range(HG)):
                for h in hs:
                    act.wait_ge(q_done, 4 * p + h + 1)
                    wait(act, keyed, 4 * p)
                    nc.scalar.activation(q[0][:, :, h, :], R[h % 2][:, :].rearrange("p (t s) -> p t s", s=S),
                                         ACT.Copy).then_inc(q_hi, 1)

            def k_split(p):
                act.wait_ge(k_done, p + 1)
                wait(act, keyed, 4 * p)
                nc.scalar.activation(k[0][:], R[0][:, :], ACT.Copy).then_inc(k_hi, 1)

            def v_split(p, par):
                act.wait_ge(vt_done, p + 1)
                wait(act, pv_done, 2 * (p - 1))
                nc.scalar.activation(v[0][:, par, :, :], R[1][:, :], ACT.Copy).then_inc(v_hi, 1)

            def v_out(p):
                act.wait_ge(v_done, p + 1)
                wait(act, vt_done, p)
                nc.scalar.activation(v_cols[:], R[1][:, :], ACT.Copy).then_inc(vt_out, 1)

            def scores_out(s):
                wait(act, scores_done, 2 * s)
                for t in range(TH):
                    act.wait_ge(keyed, 4 * s + t + 1)
                    for b in range(2):
                        rows = slice(b * S, (b + 1) * S)
                        last = nc.scalar.activation(st[rows, t, :], SC[t % 2][rows, b * 256:(b + 1) * 256], ACT.Copy)
                    last.then_inc(st_out, 1)

            def exps(s):
                act.wait_ge(shifted, s + 1)
                nc.scalar.activation(probs[:], probs[:], ACT.Exp).then_inc(exp_done, 1)

            def probs_split(s):
                wait(act, pv_done, 2 * s)
                for u in range(2):
                    act.wait_ge(pt_done, 2 * s + u + 1)
                    nc.scalar.activation(pt[0][:, u, :, :], T[u][:, :], ACT.Copy).then_inc(pt_hi, 1)

            def out_split(s, u):
                act.wait_ge(pv_done, 2 * s + u + 1)
                wait(act, y_done, 4 * s)
                for b in range(2):
                    nc.scalar.activation(out_cols(ot[0], u, b), O[b][:, :].rearrange("p (t h s) -> p t h s", t=2, h=HG),
                                         ACT.Copy).then_inc(o_hi, 1)

            def experts_hi(e):
                act.wait_ge(top["we_in"][e], 16)
                act.wait_ge(k_done, 2 * G)
                act.wait_ge(v_done, 2 * G)
                for n in range(e * C, (e + 1) * C):
                    nc.scalar.activation(we[0][:, n, :], raw[:, n, :], ACT.Copy).then_inc(top["we_hi"], 1)

            def step(s, g, hf, first=False, more=True):
                if first:
                    q_split(s + 1, (0, 1))
                exps(s)
                if hf == 0:
                    weights_hi(g, range(HG))
                if more:
                    q_split(s + 1, (2, 3) if first else range(HG))
                else:
                    experts_hi(0)
                probs_split(s)
                if more:
                    k_split(s + 1)
                out_split(s, 0)
                if more:
                    v_out(s + 1)
                out_split(s, 1)
                if more:
                    scores_out(s + 1)
                    v_split(s + 1, 1 - hf)
                else:
                    nt2.split_hi(act, EARLY, BANKS)
                    experts_hi(1)
                if hf == 0 and not (isinstance(g, int) and g == G - 1):
                    weights_hi(g, range(HG, PER))

            v_split(0, 0)
            q_split(0)
            nt.split_hi(act, LATE, BANKS)
            scores_out(0)
            step(0, 0, 0, first=True)
            step(1, 0, 1)
            with act.Fori(1, G - 1) as g:
                step(2 * g, g, 0)
                step(2 * g + 1, g, 1)
            step(2 * G - 2, G - 1, 0)
            step(2 * G - 1, G - 1, 1, more=False)

        @block.vector
        def _(dve):
            def lo(dst, src, hi, done):
                return nc.vector.tensor_tensor(dst, src, hi.bitcast(F32), ALU.subtract).then_inc(done, 1)

            def q_split(p, hs=range(HG)):
                for h in hs:
                    dve.wait_ge(q_hi, 4 * p + h + 1)
                    lo(q[1][:, :, h, :], R[h % 2][:, :].rearrange("p (t s) -> p t s", s=S), q[0][:, :, h, :], q_lo)

            def k_split(p):
                dve.wait_ge(k_hi, p + 1)
                lo(k[1][:], R[0][:, :], k[0][:], k_lo)

            def v_split(p, par):
                dve.wait_ge(v_hi, p + 1)
                lo(v[1][:, par, :, :].rearrange("p t d -> p (t d)"), R[1][:, :],
                   v[0][:, par, :, :].rearrange("p t d -> p (t d)"), v_lo)

            def probs_split(s):
                for u in range(2):
                    dve.wait_ge(pt_hi, 2 * s + u + 1)
                    lo(pt[1][:, u, :, :].rearrange("p t c -> p (t c)"), T[u][:, :],
                       pt[0][:, u, :, :].rearrange("p t c -> p (t c)"), pt_lo)

            def out_split(s, u):
                for b in range(2):
                    dve.wait_ge(o_hi, 4 * s + 2 * u + b + 1)
                    lo(out_cols(ot[1], u, b), O[b][:, :].rearrange("p (t h s) -> p t h s", t=2, h=HG),
                       out_cols(ot[0], u, b), o_lo)

            def mask_scores(s):
                wait(dve, pt_done, 2 * s)
                for u in range(2):
                    dve.wait_ge(scores_done, 2 * s + u + 1)
                    rows = probs[:, 2 * u:2 * u + 2, :, :, :].rearrange("p t r b k -> p (t r b) k")
                    nc.vector.scalar_tensor_tensor(rows, T[u][:, :].rearrange("p (n k) -> p n k", k=S), DK ** -0.5,
                                                   mask[:].unsqueeze(1).broadcast_to([P, 2 * HG, S]),
                                                   ALU.mult, ALU.add).then_inc(masked, 1)

            def row_maxima(s):
                dve.wait_ge(masked, 2 * s + 2)
                nc.vector.tensor_reduce(mx[:], probs[:].rearrange("p t r b k -> p (t r b) k"), AX.X,
                                        ALU.max).then_inc(row_max, 1)

            def invert(s):
                dve.wait_ge(exp_done, s + 1)
                nc.vector.tensor_reduce(den[:], probs[:].rearrange("p t r b k -> p (t r b) k"), AX.X,
                                        ALU.add).then_inc(summed, 1)
                dve.wait_ge(summed, s + 1)
                nc.vector.reciprocal(den[:], den[:]).then_inc(inverse, 1)

            def add_out(s, hf, ts):
                for t in ts:
                    dve.wait_ge(y_done, 4 * s + t + 1)
                    row = nt.row(hf * TH + t)
                    nc.vector.tensor_tensor(row, R[t % 2][:, :], row, ALU.add).then_inc(y_added, 1)

            def step(s, hf, first=False, more=True):
                mask_scores(s)
                if not first:
                    add_out(s - 1, 1 - hf, (0,))
                row_maxima(s)
                if first:
                    q_split(s + 1, (0, 1))
                else:
                    add_out(s - 1, 1 - hf, (1, 2))
                invert(s)
                if not first:
                    add_out(s - 1, 1 - hf, (3,))
                if more:
                    q_split(s + 1, (2, 3) if first else range(HG))
                else:
                    dve.wait_ge(y_added, 4 * s)
                    nt2.stats(dve, EARLY)
                probs_split(s)
                if more:
                    k_split(s + 1)
                out_split(s, 0)
                if not more:
                    nt2.invert(dve, EARLY)
                    nt2.norm(EARLY[0:2])
                out_split(s, 1)
                if more:
                    v_split(s + 1, 1 - hf)
                else:
                    nt2.norm(EARLY[2:])

            nt.stats(dve, [NT - 1])
            v_split(0, 0)
            nt.invert(dve, LATE)
            q_split(0, (0,))
            nt.norm(LATE)
            q_split(0, (1, 2, 3))
            nt.split_lo(dve, LATE, BANKS)
            dve.wait_ge(mask_in, 16)
            step(0, 0, first=True)
            step(1, 1)
            with dve.Fori(1, G - 1) as g:
                step(2 * g, 0)
                step(2 * g + 1, 1)
            step(2 * G - 2, 0)
            step(2 * G - 1, 1, more=False)
            for t in range(TH - 1):
                add_out(2 * G - 1, 1, [t])
                dve.wait_ge(y_added, 4 * (2 * G - 1) + t + 1)
                nt2.stats(dve, [TH + t])
                if t == 0:
                    nt2.split_lo(dve, EARLY, BANKS)
            add_out(2 * G - 1, 1, [TH - 1])

        @block.gpsimd
        def _(pool):
            def weights_lo(g, js):
                for j in js:
                    pool.wait_ge(w_hi, unit(g, j) + 1)
                    n = slot(j)[0]
                    w, at = (wd, j) if j < HG else (wq, j - HG) if j < 2 * HG else (wkv, j - 2 * HG)
                    if w is wd:
                        dst, hi = w[1][:, at, :], w[0][:, at, :]
                    else:
                        dst, hi = [w[m][:, at, :, :].rearrange("p c d -> p (c d)") for m in (1, 0)]
                    nc.gpsimd.tensor_tensor(dst, raw[:, n, :], hi.bitcast(F32), ALU.subtract).then_inc(w_lo, 1)

            def softmax(s):
                v2 = probs[:].rearrange("p t r b k -> p (t r b) k")
                pool.wait_ge(row_max, s + 1)
                nc.gpsimd.tensor_tensor(v2, v2, mx[:].unsqueeze(2).broadcast_to([P, 4 * TH, S]),
                                        ALU.subtract).then_inc(shifted, 1)
                pool.wait_ge(inverse, s + 1)
                nc.gpsimd.tensor_tensor(v2, v2, den[:].unsqueeze(2).broadcast_to([P, 4 * TH, S]),
                                        ALU.mult).then_inc(probs_done, 1)

            def step(s, g, hf):
                softmax(s)
                last = isinstance(g, int) and g == G - 1
                if hf == 0:
                    weights_lo(g, range(HG if last else 2 * HG))
                elif not last:
                    weights_lo(g, range(2 * HG, PER))

            step(0, 0, 0)
            step(1, 0, 1)
            with pool.Fori(1, G - 1) as g:
                step(2 * g, g, 0)
                step(2 * g + 1, g, 1)
            step(2 * G - 2, G - 1, 0)
            step(2 * G - 1, G - 1, 1)
            for n in range(2 * C):
                pool.wait_ge(top["we_hi"], n + 1)
                nc.gpsimd.tensor_tensor(we[1][:, n, :], raw[:, n, :], we[0][:, n, :].bitcast(F32),
                                        ALU.subtract).then_inc(top["we_lo"], 1)


def experts(nc, top, nt, nt_out, w_gate, b_gate, w_e, b_e, before, out):
    with ExitStack() as ctx:
        def sb(name, shape, dt=F32):
            return ctx.enter_context(nc.sbuf_tensor(name, shape, dt))

        def split(name, shape):
            return sb(name + "_hi", shape, F32R), sb(name + "_lo", shape, F32R)

        def sem(name):
            return ctx.enter_context(nc.semaphore(name))

        x_tok = top["x_tok"]
        xt = top["xt"]
        raw = top["raw"][:].rearrange("p (e c) d -> p e c d", e=2)
        we = [a[:, 0:2 * C, :].rearrange("p (e c) d -> p e c d", e=2) for a in top["big"]]
        wg_raw = sb("wg_raw", [P, C, E])
        wg = split("wg", [P, C, E])
        bg = sb("bg", [P, E])
        be = sb("be", [P, E * D])
        pred = sb("pred", [P, E, E])
        logits = sb("logits", [P, NT, E])
        beats = sb("beats", [P, NT, E, E])
        ties = sb("ties", [P, NT, E, E])
        rank = sb("rank", [P, NT, E])
        share = sb("share", [P, E * NT])
        cur = sb("cur", [P, 2, NT])
        gate = sb("gate", [E, TOK])
        pre = sb("pre", [P, 4, D])
        act_out = sb("act_out", [P, 4, D])

        def ps(name):
            return ctx.enter_context(nc.psum_tensor(name, [P, D], F32))

        F = [ps(f"eF{i}") for i in range(4)]
        T = [ps("eT0"), ps("eT1")]
        GT = ps("eG")
        BANKS, LATE = T + [GT, ps("eS")], range(TH, NT)

        we_in, we_hi, we_lo = top["we_in"], top["we_hi"], top["we_lo"]
        g_in, be_in = sem("g_in"), [sem("be_in0"), sem("be_in1")]
        wg_hi, wg_lo = sem("wg_hi"), sem("wg_lo")
        gate_cols, gate_out, gate_done, chosen = sem("gate_cols"), sem("gate_out"), sem("gate_done"), sem("chosen")
        item_done, biased, relu_done, added = sem("item_done"), sem("biased"), sem("relu_done"), sem("added")
        picked, added_pool = sem("picked"), sem("added_pool")
        step_d = sem("step_d")
        row_out = sem("row_out")

        block = ctx.enter_context(nc.Block())

        @block.sync
        def _(sp):
            def load(e, par):
                wait(sp, we_lo, C * (e - 1))
                sp.dma_start(raw[:, par, :, :], w_e[e].rearrange("c p h -> p c h")).then_inc(we_in[par], 16)

            sp.dma_start(be[:, 0:D], b_e[:, 0:D].to_broadcast([P, D])).then_inc(be_in[0], 16)
            sp.dma_start(wg_raw[:], w_gate).then_inc(g_in, 16)
            sp.dma_start(bg[:], b_gate.to_broadcast([P, E])).then_inc(g_in, 16)
            sp.dma_start(pred[:], before).then_inc(g_in, 16)
            sp.dma_start(be[:, D:], b_e[:, D:].to_broadcast([P, (E - 1) * D])).then_inc(be_in[1], 16)
            with sp.Fori(1, E // 2) as n:
                load(2 * n, 0)
                load(2 * n + 1, 1)
            for t in range(NT):
                if t < NT - 2:
                    sp.wait_ge(nt_out.normed_act, t + 1)
                else:
                    sp.wait_ge(nt_out.normed, t - (NT - 2) + 1)
                sp.dma_start(out[t], x_tok[:, t * D:(t + 1) * D]).then_inc(row_out, 16)
            sp.wait_ge(row_out, 16 * NT)

        @block.tensor
        def _(pe):
            def gate_rows():
                pe.wait_ge(nt.lo, NT)
                pe.wait_ge(wg_lo, 1)
                for hf in range(2):
                    for c in range(C):
                        last = products(nc, T[hf][0:E, :], [a[:, c, :] for a in wg],
                                        [a[:, c, hf * HALF:(hf + 1) * HALF] for a in xt],
                                        start=(c == 0), stop=(c == C - 1))
                last.then_inc(gate_cols, 1)

            def turn_gate():
                pe.wait_ge(gate_out, 1)
                for t in range(NT):
                    last = nc.tensor.transpose(GT[:, t * E:(t + 1) * E], gate[:, t * P:(t + 1) * P], top["ident"][0:E, 0:E])
                last.then_inc(gate_done, 1)

            def expert(e, par, first=False):
                pe.wait_ge(we_lo, C * (e + 1))
                for t in range(NT):
                    if first and t == 2:
                        nt.turn(pe, LATE, BANKS)
                    if first and t == 4:
                        gate_rows()
                    if first and t == 5:
                        turn_gate()
                    wait(pe, biased, NT * e + t - 3)
                    for c in range(C):
                        last = products(nc, F[t % 4][:, :], [a[:, c, t * P:(t + 1) * P] for a in xt],
                                        [a[:, par, c, :] for a in we], start=(c == 0), stop=(c == C - 1))
                    last.then_inc(item_done, 1)

            expert(0, 0, first=True)
            expert(1, 1)
            with pe.Fori(1, E // 2) as n:
                expert(2 * n, 0)
                expert(2 * n + 1, 1)

        @block.scalar
        def _(act):
            def weights_hi(n, par):
                act.wait_ge(we_in[par], 16 * n + 16)
                wait(act, item_done, NT * (2 * n + par - 1))
                for c in range(C):
                    nc.scalar.activation(we[0][:, par, c, :], raw[:, par, c, :], ACT.Copy).then_inc(we_hi, 1)

            def relus(e, par, last=False):
                for t in range(NT):
                    if last and t == NT - 1:
                        act.wait_ge(nt_out.shifted, 1)
                        nt_out.norm_act(range(0, 2), nt_out.normed_act)
                    act.wait_ge(biased, NT * e + t + 1)
                    if t == 0:
                        act.wait_ge(picked, e + 1)
                    if last and t >= 4:
                        act.wait_ge(added_pool, t - 3)
                    else:
                        wait(act, added, NT * e + t - 3)
                    nc.scalar.activation(act_out[:, t % 4, :], pre[:, t % 4, :], ACT.Relu,
                                         scale=cur[:, par, t:t + 1]).then_inc(relu_done, 1)

            act.wait_ge(g_in, 48)
            nc.scalar.activation(wg[0][:], wg_raw[:], ACT.Copy).then_inc(wg_hi, 1)
            nt.split_hi(act, LATE, BANKS)

            act.wait_ge(gate_cols, 1)
            for hf in range(2):
                last = nc.scalar.activation(gate[:, hf * HALF:(hf + 1) * HALF], T[hf][0:E, :], ACT.Copy)
            last.then_inc(gate_out, 1)

            def pair(n, load=True):
                relus(2 * n, 0)
                if load:
                    weights_hi(n + 1, 0)
                relus(2 * n + 1, 1, last=not load)
                if load:
                    weights_hi(n + 1, 1)

            pair(0)
            with act.Fori(1, E // 2 - 1) as n:
                pair(n)
            pair(E // 2 - 1, load=False)
            nt_out.norm_act(range(2, TH), nt_out.normed_act)
            act.wait_ge(nt_out.shifted, 2)
            nt_out.norm_act(range(TH, NT - 2), nt_out.normed_act)

        @block.vector
        def _(dve):
            chain = Chain(dve, step_d, 0)

            def bias(e, t):
                dve.wait_ge(item_done, NT * e + t + 1)
                wait(dve, relu_done, NT * e + t - 3)
                nc.vector.tensor_tensor(pre[:, t % 4, :], F[t % 4][:, :], be[:, bass.ds(e * D, D)],
                                        ALU.add).then_inc(biased, 1)

            def add(e, t):
                dve.wait_ge(relu_done, NT * e + t + 1)
                row = nt.row(t)
                nc.vector.tensor_tensor(row, act_out[:, t % 4, :], row, ALU.add).then_inc(added, 1)

            def pick(e, par):
                wait(dve, relu_done, NT * (e - 1))
                nc.vector.tensor_copy(cur[:, par, :], share[:, bass.ds(e * NT, NT)]).then_inc(picked, 1)

            def choose():
                dve.wait_ge(gate_done, 1)
                chain.link(nc.vector.tensor_tensor(logits[:], GT[:, 0:NT * E].rearrange("p (t e) -> p t e", e=E),
                                                   bg[:].unsqueeze(1).broadcast_to([P, NT, E]), ALU.add))
                mine = logits[:].unsqueeze(3).broadcast_to([P, NT, E, E])
                other = logits[:].unsqueeze(2).broadcast_to([P, NT, E, E])
                nc.vector.tensor_tensor(beats[:], other, mine, ALU.is_gt)
                chain.link(nc.vector.tensor_tensor(ties[:], other, mine, ALU.is_equal))
                chain.link(nc.vector.tensor_tensor(ties[:], ties[:], pred[:].unsqueeze(1).broadcast_to([P, NT, E, E]),
                                                   ALU.mult))
                chain.link(nc.vector.tensor_tensor(beats[:], beats[:], ties[:], ALU.add))
                chain.link(nc.vector.tensor_reduce(rank[:], beats[:], AX.X, ALU.add))
                nc.vector.tensor_scalar(share[:].rearrange("p (e t) -> p t e", t=NT), rank[:], 1.5, 0.5,
                                        ALU.is_lt, ALU.mult).then_inc(chosen, 1)
                dve.wait_ge(chosen, 1)

            def expert(e, par, last=False):
                pick(e, par)
                for t in range(NT):
                    bias(e, t)
                    if t < 2:
                        add(e - 1, t + NT - 2)
                    elif last:
                        dve.wait_ge(added_pool, t - 1)
                        nt_out.stats(dve, [t - 2])
                    else:
                        add(e, t - 2)
                    if last and t == TH + 1:
                        nt_out.invert(dve, range(TH))
                        nt_out.shift(range(TH))

            nt.stats(dve, [NT - 1])
            nt.invert(dve, LATE)
            nt.norm(LATE)
            dve.wait_ge(g_in, 48)
            dve.wait_ge(wg_hi, 1)
            nc.vector.tensor_tensor(wg[1][:], wg_raw[:], wg[0][:].bitcast(F32), ALU.subtract).then_inc(wg_lo, 1)
            dve.wait_ge(be_in[0], 16)
            bias(0, 0)
            bias(0, 1)
            nt.split_lo(dve, LATE, BANKS)
            bias(0, 2)
            bias(0, 3)
            choose()
            pick(0, 0)
            for t in range(4, NT):
                bias(0, t)
                for done in ((0,), (1, 2), (3, 4), (5,))[t - 4]:
                    add(0, done)
            dve.wait_ge(be_in[1], 16)
            expert(1, 1)
            with dve.Fori(1, E // 2 - 1) as n:
                expert(2 * n, 0)
                expert(2 * n + 1, 1)
            expert(E - 2, 0)
            expert(E - 1, 1, last=True)
            dve.wait_ge(added_pool, NT - 1)
            nt_out.stats(dve, [NT - 2])
            add(E - 1, NT - 1)
            dve.wait_ge(added, NT * (E - 1) + 1)
            nt_out.stats(dve, [NT - 1])
            nt_out.invert(dve, range(TH, NT))
            nt_out.shift(range(TH, NT))
            nt_out.norm(range(NT - 2, NT))

        @block.gpsimd
        def _(pool):
            def weights_lo(e, par):
                for c in range(C):
                    pool.wait_ge(we_hi, C * e + c + 1)
                    nc.gpsimd.tensor_tensor(we[1][:, par, c, :], raw[:, par, c, :], we[0][:, par, c, :].bitcast(F32),
                                            ALU.subtract).then_inc(we_lo, 1)

            with pool.Fori(1, E // 2) as n:
                weights_lo(2 * n, 0)
                weights_lo(2 * n + 1, 1)
            for t in range(NT - 1):
                pool.wait_ge(relu_done, NT * (E - 1) + t + 1)
                pool.wait_ge(added, NT * (E - 2) + t + 1)
                row = nt.row(t)
                nc.gpsimd.tensor_tensor(row, act_out[:, t % 4, :], row, ALU.add).then_inc(added_pool, 1)


def program(nc, io, out):
    with ExitStack() as ctx:
        def split(name, shape):
            return [ctx.enter_context(nc.sbuf_tensor(f"{name}_{part}", shape, F32R)) for part in ("hi", "lo")]

        top = {
            "x_tok": ctx.enter_context(nc.sbuf_tensor("x_tok", [P, NT * D], F32)),
            "ident": ctx.enter_context(nc.sbuf_tensor("ident", [P, P], F32)),
            "raw": ctx.enter_context(nc.sbuf_tensor("raw", [P, SLOTS, D], F32)),
            "xt": split("x_cols", [P, C, TOK]),
            "big": split("big", [P, 3 * C, D]),
            "wkv": split("wkv", [P, 2, C * DK]),
            "k": split("k", [P, HALF]),
            "v_cols": ctx.enter_context(nc.sbuf_tensor("v_cols", [P, HALF], F32)),
            **{name: ctx.enter_context(nc.semaphore(name)) for name in ("k_done", "v_done", "k_hi", "k_lo", "vt_out")},
            "we_in": [ctx.enter_context(nc.semaphore(f"we_in{e}")) for e in range(2)],
            "we_hi": ctx.enter_context(nc.semaphore("we_hi")),
            "we_lo": ctx.enter_context(nc.semaphore("we_lo")),
        }
        ln1, ln2, ln3 = [NormTurn(nc, ctx, name, top) for name in ("ln1", "ln2", "ln3")]
        self_attention(nc, top, ln1, io["x_rows"], io["x_cols"], io["w_qkv"], io["w_out"], io["ln_cols"],
                       io["alibi"], io["head_rows"], io["ctx_cols"], io["w_q"], io["w_kv"])
        cross_attention(nc, top, ln1, ln2, io["w_q"], io["w_kv"], io["w_d"], io["causal"], io["w_e"])
        experts(nc, top, ln2, ln3, io["w_gate"], io["b_gate"], io["w_e"], io["b_e"], io["before"], out)


def kernel(x, ctx_4096, L0_attn_Wqkv, L0_attn_q_ln_w, L0_attn_q_ln_b, L0_attn_k_ln_w, L0_attn_k_ln_b,
           L0_attn_Wout, L0_xattn_Wq, L0_xattn_Wk, L0_xattn_Wv, L0_xattn_Wd, L0_ffn_W_gate, L0_ffn_b_gate,
           L0_ffn_W_e, L0_ffn_b_e):
    import numpy as np
    import concourse.bacc as bacc
    from concourse.bass_utils import run_bass_kernel_spmd

    a = np.asarray
    rows = a(x).reshape(NT, P, D)
    slopes = 1.0 / np.power(2.0, np.arange(1, NH + 1, dtype=np.float32) * (8.0 / NH))
    rel = (np.arange(S)[None, :] - (np.arange(P) % S)[:, None]).astype(np.float32)
    hidden = np.where(rel <= 0, np.float32(0), np.float32(-1e30))
    alibi = np.where(rel[:, None, :] <= 0, slopes[None, :, None] * rel[:, None, :], np.float32(-1e30))
    lay = {
        "x_rows": rows.transpose(1, 0, 2),
        "x_cols": rows.reshape(NT, P, C, P).transpose(0, 3, 2, 1),
        "w_qkv": a(L0_attn_Wqkv).reshape(3, D, C, P).transpose(0, 2, 3, 1).reshape(3 * C, P, D),
        "w_out": a(L0_attn_Wout).reshape(D, C, P).transpose(1, 2, 0),
        "ln_cols": np.stack([a(v).reshape(C, P).T for v in
                             (L0_attn_q_ln_w, L0_attn_q_ln_b, L0_attn_k_ln_w, L0_attn_k_ln_b)], axis=1),
        "alibi": alibi.astype(np.float32),
        "causal": hidden.astype(np.float32),
        "head_rows": (np.arange(P)[:, None] // HD == np.arange(HPC)[None, :]).astype(np.float32),
        "before": np.broadcast_to((np.arange(E)[None, :] < np.arange(E)[:, None]).astype(np.float32), (P, E, E)),
        "ctx_cols": a(ctx_4096).reshape(2, HALF, C, P).transpose(2, 0, 3, 1),
        "w_q": a(L0_xattn_Wq).reshape(G, HG, DK, C, P).transpose(0, 1, 4, 3, 2).reshape(G, HG, P, C * DK),
        "w_kv": np.stack([a(w).reshape(G, DK, C, P).transpose(0, 3, 2, 1).reshape(G, P, C * DK)
                          for w in (L0_xattn_Wk, L0_xattn_Wv)], axis=1),
        "w_d": a(L0_xattn_Wd).reshape(D, G, HG, DK).transpose(1, 2, 3, 0),
        "w_gate": a(L0_ffn_W_gate).reshape(C, P, E).transpose(1, 0, 2),
        "b_gate": a(L0_ffn_b_gate).reshape(1, E),
        "w_e": a(L0_ffn_W_e).reshape(E, C, P, D),
        "b_e": a(L0_ffn_b_e).reshape(1, E * D),
    }
    nc = bacc.Bacc("TRN2", target_bir_lowering=False, num_devices=1)
    arrays, io = {}, {}
    for name, v in lay.items():
        arrays["in_" + name] = np.ascontiguousarray(v)
        io[name] = nc.dram_tensor("in_" + name, v.shape, F32, kind="ExternalInput").ap()
    out = nc.dram_tensor("out", (TOK, D), F32, kind="ExternalOutput").ap()
    program(nc, io, out.rearrange("(t p) d -> t p d", p=P))
    r = run_bass_kernel_spmd(nc, [arrays], core_ids=[0])
    return r.results[0]["out"].reshape(B, S, D)
```
